# Optimizing a Trainium2 kernel written in Bass

```python
import numpy as np
import jax
import jax.numpy as jnp

def _softmax(x, axis=-1):
    return jax.nn.softmax(x, axis=axis)

def _gelu(x):
    return jax.nn.gelu(x, approximate=True)

def _silu(x):
    return jax.nn.silu(x)

def _sigmoid(x):
    return jax.nn.sigmoid(x)

def _layernorm(x, axis=-1, eps=1e-05):
    m = jnp.mean(x, axis=axis, keepdims=True)
    v = jnp.var(x, axis=axis, keepdims=True)
    return (x - m) / jnp.sqrt(v + eps)

def _scatter_add(tgt, idx, src, axis=0):
    return tgt.at[idx].add(src)

def _segment_sum(src, seg, n):
    return jax.ops.segment_sum(src, seg, n)
kernel_name = 'mk_lm_tower_d1_tok_ids768_r4_1a2ed3'

def setup_inputs(seed: int=0):
    np.random.seed(seed)
    _w = jnp.asarray

    def _rec_inputs():
        import jax
        import jax.numpy as jnp
        _rk = jax.random.key(seed)
        x = jax.random.randint(jax.random.fold_in(_rk, 1), (16, 128), 0, 128, jnp.int32)
        mask_BS_i1_0 = jnp.where(jnp.ones((16, 128), dtype=bool), 1, 0).astype(jnp.int32)
        return (x, mask_BS_i1_0)
    x, mask_BS_i1_0 = _rec_inputs()

    def _L0_tok_setup():
        import jax, jax.numpy as jnp
        import numpy as np
        VOCAB = 8000
        D_MODEL = 192
        MAX_LEN = 128
        TYPE_VOCAB = 2
        PADDING_IDX = 1
        LN_EPS = 1e-12
        key = jax.random.key(seed)
        k1, k2, k3, k4, k5, k6 = jax.random.split(key, 6)
        B, S = (8, 1024)
        x = jax.random.randint(k1, (B, S), 0, MAX_LEN, dtype=jnp.int64)
        token_type_ids = jax.random.randint(k2, (B, S), 0, TYPE_VOCAB, dtype=jnp.int64)
        tok_table = jax.random.normal(k3, (VOCAB, D_MODEL), dtype=jnp.float32) * 0.02
        tok_table = tok_table.at[PADDING_IDX].set(0.0)
        pos_table = jax.random.normal(k4, (MAX_LEN, D_MODEL), dtype=jnp.float32) * 0.02
        type_table = jax.random.normal(k5, (TYPE_VOCAB, D_MODEL), dtype=jnp.float32) * 0.02
        gamma = jnp.ones((D_MODEL,), dtype=jnp.float32)
        beta = jnp.zeros((D_MODEL,), dtype=jnp.float32)
        return {'x': x, 'token_type_ids': token_type_ids, 'tok_table': tok_table, 'pos_table': pos_table, 'type_table': type_table, 'gamma': gamma, 'beta': beta}
    _L0_tok_all = _L0_tok_setup()
    _L0_tok_in = {k: v for k, v in _L0_tok_all.items() if k in ('tok_table', 'pos_table', 'type_table', 'gamma', 'beta')}
    del _L0_tok_all

    def _L0_attn_setup():
        import jax, jax.numpy as jnp
        import numpy as np
        import math
        B, L, DM = (4, 512, 192)
        H = 12
        FD = 16
        HD = DM // H
        EPS = 1e-12
        CHUNK = 128

        def taylor_exp(x):
            d = x.shape[-1]
            r2 = math.sqrt(2.0)
            rd = math.sqrt(float(d))
            rrd = math.sqrt(rd)
            x2 = (x[..., :, None] * x[..., None, :]).reshape(x.shape[:-1] + (d * d,)) / r2
            ones = jnp.ones(x.shape[:-1] + (1,), dtype=x.dtype)
            return jnp.concatenate([ones, x / rrd, x2 / rd], axis=-1)

        def linear_attn_causal(q, k, v, eps):
            b, h, l, D = q.shape
            e = v.shape[-1]
            n = l // CHUNK
            qc = q.reshape(b, h, n, CHUNK, D).transpose(2, 0, 1, 3, 4)
            kc = k.reshape(b, h, n, CHUNK, D).transpose(2, 0, 1, 3, 4)
            vc = v.reshape(b, h, n, CHUNK, e).transpose(2, 0, 1, 3, 4)
            mask = jnp.tril(jnp.ones((CHUNK, CHUNK), dtype=q.dtype))

            def step(carry, xs):
                S, s = carry
                qi, ki, vi = xs
                inner = jnp.einsum('bhcd,bhmd->bhcm', qi, ki) * mask
                num = jnp.einsum('bhcd,bhde->bhce', qi, S) + jnp.einsum('bhcm,bhme->bhce', inner, vi)
                den = jnp.einsum('bhcd,bhd->bhc', qi, s) + jnp.einsum('bhcd,bhcd->bhc', qi, jnp.cumsum(ki, axis=2))
                S = S + jnp.einsum('bhcd,bhce->bhde', ki, vi)
                s = s + ki.sum(axis=2)
                return ((S, s), num / (den + eps)[..., None])
            S0 = jnp.zeros((b, h, D, e), dtype=q.dtype)
            s0 = jnp.zeros((b, h, D), dtype=q.dtype)
            _, y = jax.lax.scan(step, (S0, s0), (qc, kc, vc))
            return y.transpose(1, 2, 0, 3, 4).reshape(b, h, l, e)
        key = jax.random.key(seed)
        k0, k1, k2, k3, k4 = jax.random.split(key, 5)
        hidden_states = jax.random.normal(k0, (B, L, DM), dtype=jnp.float32)
        scale = 1.0 / math.sqrt(DM)
        Wq = jax.random.normal(k1, (DM, H * FD), dtype=jnp.float32) * scale
        Wk = jax.random.normal(k2, (DM, H * FD), dtype=jnp.float32) * scale
        Wv = jax.random.normal(k3, (DM, H * HD), dtype=jnp.float32) * scale
        Wo = jax.random.normal(k4, (H * HD, DM), dtype=jnp.float32) * scale
        return {'hidden_states': hidden_states, 'Wq': Wq, 'Wk': Wk, 'Wv': Wv, 'Wo': Wo}
    _L0_attn_all = _L0_attn_setup()
    _L0_attn_in = {k: v for k, v in _L0_attn_all.items() if k in ('Wq', 'Wk', 'Wv', 'Wo')}
    del _L0_attn_all

    def _L0_ffn_setup():
        import jax, jax.numpy as jnp
        import numpy as np
        B, M, D = (32, 196, 192)
        N, P, H = (64, 1, 768)
        EPS = 1e-12

        def _l2norm(v, axis):
            n = jnp.sqrt(jnp.sum(v * v, axis=axis, keepdims=True))
            return v / jnp.maximum(n, EPS)
        key = jax.random.key(seed)
        ks = jax.random.split(key, 7)
        x = jax.random.normal(ks[0], (B, M, D), dtype=jnp.float32)
        phi = jax.random.normal(ks[1], (D, N, P), dtype=jnp.float32) * (1.0 / D ** 0.5)
        scale = jnp.ones((1,), dtype=jnp.float32)
        w1 = jax.random.normal(ks[2], (N, D, H), dtype=jnp.float32) * (1.0 / D ** 0.5)
        b1 = jnp.zeros((N, H), dtype=jnp.float32)
        w2 = jax.random.normal(ks[3], (N, H, D), dtype=jnp.float32) * (1.0 / H ** 0.5)
        b2 = jnp.zeros((N, D), dtype=jnp.float32)
        return {'x': x, 'phi': phi, 'scale': scale, 'w1': w1, 'b1': b1, 'w2': w2, 'b2': b2}
    _L0_ffn_all = _L0_ffn_setup()
    _L0_ffn_in = {k: v for k, v in _L0_ffn_all.items() if k in ('phi', 'scale', 'w1', 'b1', 'w2', 'b2')}
    del _L0_ffn_all
    return {'x': x, 'mask_BS_i1_0': mask_BS_i1_0, 'L0_tok_tok_table': _L0_tok_in['tok_table'], 'L0_tok_pos_table': _L0_tok_in['pos_table'], 'L0_tok_type_table': _L0_tok_in['type_table'], 'L0_tok_gamma': _L0_tok_in['gamma'], 'L0_tok_beta': _L0_tok_in['beta'], 'L0_attn_Wq': _L0_attn_in['Wq'], 'L0_attn_Wk': _L0_attn_in['Wk'], 'L0_attn_Wv': _L0_attn_in['Wv'], 'L0_attn_Wo': _L0_attn_in['Wo'], 'L0_ffn_phi': _L0_ffn_in['phi'], 'L0_ffn_scale': _L0_ffn_in['scale'], 'L0_ffn_w1': _L0_ffn_in['w1'], 'L0_ffn_b1': _L0_ffn_in['b1'], 'L0_ffn_w2': _L0_ffn_in['w2'], 'L0_ffn_b2': _L0_ffn_in['b2']}

def reference(x, mask_BS_i1_0, L0_tok_tok_table, L0_tok_pos_table, L0_tok_type_table, L0_tok_gamma, L0_tok_beta, L0_attn_Wq, L0_attn_Wk, L0_attn_Wv, L0_attn_Wo, L0_ffn_phi, L0_ffn_scale, L0_ffn_w1, L0_ffn_b1, L0_ffn_w2, L0_ffn_b2):
    import jax
    import jax.numpy as jnp

    def _L0_tok_ref(x, token_type_ids, tok_table, pos_table, type_table, gamma, beta):
        import jax, jax.numpy as jnp
        import numpy as np
        VOCAB = 8000
        D_MODEL = 192
        MAX_LEN = 128
        TYPE_VOCAB = 2
        PADDING_IDX = 1
        LN_EPS = 1e-12
        emb = tok_table[x] + pos_table[x] + type_table[token_type_ids]
        mean = jnp.mean(emb, axis=-1, keepdims=True)
        var = jnp.mean(jnp.square(emb - mean), axis=-1, keepdims=True)
        out = (emb - mean) * jax.lax.rsqrt(var + LN_EPS) * gamma + beta
        return out

    def _L0_attn_ref(hidden_states, Wq, Wk, Wv, Wo):
        import jax, jax.numpy as jnp
        import numpy as np
        import math
        B, L, DM = (4, 512, 192)
        H = 12
        FD = 16
        HD = DM // H
        EPS = 1e-12
        CHUNK = 128

        def taylor_exp(x):
            d = x.shape[-1]
            r2 = math.sqrt(2.0)
            rd = math.sqrt(float(d))
            rrd = math.sqrt(rd)
            x2 = (x[..., :, None] * x[..., None, :]).reshape(x.shape[:-1] + (d * d,)) / r2
            ones = jnp.ones(x.shape[:-1] + (1,), dtype=x.dtype)
            return jnp.concatenate([ones, x / rrd, x2 / rd], axis=-1)

        def linear_attn_causal(q, k, v, eps):
            b, h, l, D = q.shape
            e = v.shape[-1]
            n = l // CHUNK
            qc = q.reshape(b, h, n, CHUNK, D).transpose(2, 0, 1, 3, 4)
            kc = k.reshape(b, h, n, CHUNK, D).transpose(2, 0, 1, 3, 4)
            vc = v.reshape(b, h, n, CHUNK, e).transpose(2, 0, 1, 3, 4)
            mask = jnp.tril(jnp.ones((CHUNK, CHUNK), dtype=q.dtype))

            def step(carry, xs):
                S, s = carry
                qi, ki, vi = xs
                inner = jnp.einsum('bhcd,bhmd->bhcm', qi, ki) * mask
                num = jnp.einsum('bhcd,bhde->bhce', qi, S) + jnp.einsum('bhcm,bhme->bhce', inner, vi)
                den = jnp.einsum('bhcd,bhd->bhc', qi, s) + jnp.einsum('bhcd,bhcd->bhc', qi, jnp.cumsum(ki, axis=2))
                S = S + jnp.einsum('bhcd,bhce->bhde', ki, vi)
                s = s + ki.sum(axis=2)
                return ((S, s), num / (den + eps)[..., None])
            S0 = jnp.zeros((b, h, D, e), dtype=q.dtype)
            s0 = jnp.zeros((b, h, D), dtype=q.dtype)
            _, y = jax.lax.scan(step, (S0, s0), (qc, kc, vc))
            return y.transpose(1, 2, 0, 3, 4).reshape(b, h, l, e)
        b, l, _ = hidden_states.shape
        q = (hidden_states @ Wq).reshape(b, l, H, FD).transpose(0, 2, 1, 3)
        k = (hidden_states @ Wk).reshape(b, l, H, FD).transpose(0, 2, 1, 3)
        v = (hidden_states @ Wv).reshape(b, l, H, HD).transpose(0, 2, 1, 3)
        q = taylor_exp(q)
        k = taylor_exp(k)
        y = linear_attn_causal(q, k, v, EPS)
        y = y.transpose(0, 2, 1, 3).reshape(b, l, H * HD)
        return y @ Wo

    def _L0_ffn_ref(x, phi, scale, w1, b1, w2, b2):
        import jax, jax.numpy as jnp
        import numpy as np
        B, M, D = (32, 196, 192)
        N, P, H = (64, 1, 768)
        EPS = 1e-12

        def _l2norm(v, axis):
            n = jnp.sqrt(jnp.sum(v * v, axis=axis, keepdims=True))
            return v / jnp.maximum(n, EPS)
        xn = _l2norm(x, axis=2)
        phin = scale * _l2norm(phi, axis=0)
        logits = jnp.einsum('bmd,dnp->bmnp', xn, phin)
        d = jax.nn.softmax(logits, axis=1)
        b_, m_, n_, p_ = logits.shape
        c = jax.nn.softmax(logits.reshape(b_, m_, n_ * p_), axis=-1).reshape(b_, m_, n_, p_)
        xs = jnp.einsum('bmd,bmnp->bnpd', xn, d)
        h = jax.nn.gelu(jnp.einsum('bnpd,ndh->bnph', xs, w1) + b1[None, :, None, :], approximate=False)
        ys = jnp.einsum('bnph,nhd->bnpd', h, w2) + b2[None, :, None, :]
        y = jnp.einsum('bnpd,bmnp->bmd', ys, c)
        return y
    h = _L0_tok_ref(x, mask_BS_i1_0, L0_tok_tok_table, L0_tok_pos_table, L0_tok_type_table, L0_tok_gamma, L0_tok_beta)
    h = h + _L0_attn_ref(_layernorm(h, axis=-1), L0_attn_Wq, L0_attn_Wk, L0_attn_Wv, L0_attn_Wo)
    h = h + _L0_ffn_ref(_layernorm(h, axis=-1), L0_ffn_phi, L0_ffn_scale, L0_ffn_w1, L0_ffn_b1, L0_ffn_w2, L0_ffn_b2)
    return h

_drawn_inputs = setup_inputs


def setup_inputs(seed=0):
    import zlib

    import numpy as np

    out = dict(_drawn_inputs(seed))
    spreads = {'L0_tok_gamma': (1.0, 0.2),
     'L0_tok_beta': (0.0, 0.1),
     'L0_ffn_b1': (0.0, 0.8),
     'L0_ffn_b2': (0.0, 0.784)}
    factors = {'L0_ffn_phi': 8.0, 'L0_ffn_w1': 8.0, 'L0_ffn_w2': 8.0}
    for name, (base, spread) in spreads.items():
        noise = np.random.default_rng([zlib.crc32(name.encode()), seed]).standard_normal(out[name].shape)
        drawn = base * np.exp(spread * noise) if base else spread * noise
        out[name] = jnp.asarray(drawn.astype(out[name].dtype))
    for name, factor in factors.items():
        out[name] = (out[name] * factor).astype(out[name].dtype)
    return out
```

```python
from contextlib import ExitStack

import concourse.bass as bass
from concourse import mybir

F32 = mybir.dt.float32
I32 = mybir.dt.int32
U32 = mybir.dt.uint32
ACT = mybir.ActivationFunctionType
ALU = mybir.AluOpType
AX = mybir.AxisListType

P = 128
B, S = 16, 128
D = 192
HD = D // 2
H, FD = 12, 16
HH = H // 2
NE, F = 64, 768
NQ, J = 4, 4
NPAIR = NE // 2
G = 8
NG = NE // G
GP = G // 2
KT1 = 2 * D // P
KT2 = F // P
SLOTS = 2 * GP
W1C = KT1 * F
W2C = 2 * KT2 * D
SLOT = W1C + W2C
TABLES = (8000, 128, 2)
MAGIC = float(0x5F3759DF)

PROJECT = ["XT0", "XT1", "QK0", "QK1", "QK2", "QK3", "V0", "V1"]
ORDER = ["S0", "S1", "PV0", "S2", "YT0", "PV1", "YN0", "S3", "WO0", "YT1", "PV2", "YN1", "XT0'", "XT1'", "WO1",
         "YT2", "PV3", "YN2", "QK0'", "WO2", "YT3", "QK1'", "YN3", "QK2'", "WO3", "QK3'", "XN0", "XN1", "V0'",
         "LT", "V1'", "LN", "DT", "XS", "CT"]
SHARED = ("XT", "QK", "V0", "V1", "XN", "LT", "LN", "DT", "XS", "CT")


def shared_uses(order):
    seen, found = [0, 0], {}
    for stage in [s for s in order if s.startswith(SHARED)]:
        bank = len(found) % 2
        found[stage] = (bank, seen[bank])
        seen[bank] += 1
    return found, seen


def tower_kernel(nc, x, types, tok_table, pos_table, type_table, gamma, beta, wq, wk, wv, wo, phi, scale,
                 w1, b1, w2, b2, out):
    with ExitStack() as ctx:
        def sb(name, cols, parts=P):
            return ctx.enter_context(nc.sbuf_tensor(name, [parts, cols], F32))

        def sem(name):
            return ctx.enter_context(nc.semaphore(name))

        ring = sb("ring", SLOTS * SLOT)
        hidden = sb("hidden", B * D)[:, :].rearrange("p (b d) -> p b d", b=B)
        slots_t = sb("slots_t", KT1 * NPAIR * 32)[:, :].rearrange("p (k n c) -> p k n c", k=KT1, n=NPAIR)
        combine_t = sb("combine_t", B * S)[:, :].rearrange("p (b m) -> p b m", b=B)
        ident = sb("ident", P)[:, :]
        b1_t = sb("b1_t", KT2 * NE)[:, :].rearrange("p (t n) -> p t n", t=KT2)
        odd = sb("odd", 1)[:, :].bitcast(I32)
        late = sb("late", 3072 + 3456)

        def carve(tensor, at, sizes):
            views = []
            for n in sizes:
                views.append(tensor[:, at:at + n])
                at += n
            return views, at

        (slot_out, h_sb, h_t, act_t, staged0, staged1, y_sb0, y_sb1), _ = carve(
            late, 0, [B * D, F, F, F, KT1 * GP * 32, KT1 * GP * 32, D, D])
        slot_out = slot_out.rearrange("p (b d) -> p b d", b=B)
        h_sb = h_sb.rearrange("p (t c) -> p t c", t=KT2)
        h_t = h_t.rearrange("p (t e b) -> p t e b", t=KT2, e=G)
        act_t = act_t.rearrange("p (t r) -> p t r", t=KT2)
        staged = [s.rearrange("p (k n c) -> p k n c", k=KT1, n=GP) for s in (staged0, staged1)]
        y_sb = [y_sb0, y_sb1]

        def w1_slot(k):
            return ring[:, k * SLOT:k * SLOT + W1C].rearrange("p (k f) -> p k f", k=KT1)

        def w2_slot(k):
            return ring[:, k * SLOT + W1C:(k + 1) * SLOT].rearrange("p (e t d) -> p e t d", e=2, t=KT2)

        EARLY_SLOT = 5
        (emb, xa, xa_t, q_t, k_t, q_diag, v_aug, probs, xn_t), end = carve(
            ring, EARLY_SLOT * SLOT, [3 * J * D, J * D, 2 * J * S, 2 * J * S, 2 * J * S, H * S, J * H * 32,
                                      2 * H * S, 2 * J * S])
        assert end <= SLOTS * SLOT
        (ids, phi_sq, phi_w, b1_sb), _ = carve(probs, 0, [6 * S, 2 * NE, 4 * NE, F])
        (pv_sb, yn, yn_t, exp_d, log_t, disp, disp_t, log_c, exp_c, comb, w_qkv, w_o, mask, head_mask, phi_sb,
         phi_n, gam, bet, small, ones, xn), end = carve(
            late, 0, [3 * S, D, 2 * S, 256, 256, 256, 256, 256, 256, 512, 2 * 3 * D, 2 * D, S, HH, 2 * NE,
                      2 * NE, D, D, 192, HD, J * D])
        assert end <= 3072 + 3456, end
        emb = emb.rearrange("p (t j d) -> p t j d", t=3, j=J)
        xa = xa.rearrange("p (j d) -> p j d", j=J)
        xa_t = xa_t.rearrange("p (c m) -> p c m", c=2)
        q_t = q_t.rearrange("p (c m) -> p c m", c=2)
        k_t = k_t.rearrange("p (c m) -> p c m", c=2)
        q_diag = q_diag.rearrange("p (g h m) -> p g h m", g=2, h=HH)
        v_aug = v_aug.rearrange("p (j h e) -> p j h e", j=J, h=H)
        probs = probs.rearrange("p (u h m) -> p u h m", u=2, h=H)
        xn = xn.rearrange("p (j d) -> p j d", j=J)
        xn_t = xn_t.rearrange("p (c m) -> p c m", c=2)
        yn_t = yn_t.rearrange("p (c m) -> p c m", c=2)
        exp_d, log_t, disp = (a.rearrange("p (i m) -> p i m", i=2) for a in (exp_d, log_t, disp))
        disp_t, log_c, exp_c = (a.rearrange("p (j n) -> p j n", j=J) for a in (disp_t, log_c, exp_c))
        comb = comb.rearrange("p (j r n) -> p j r n", j=J, r=2)
        w_qkv = w_qkv.rearrange("p (c n) -> p c n", c=2)
        w_o = w_o[0:HD, :].rearrange("p (c n) -> p c n", c=2)
        ids_f = ids[:, 2 * S:5 * S].rearrange("p (t m) -> p t m", t=3)
        ids_w = ids[:, 5 * S:6 * S]
        phi_n2 = phi_n.rearrange("p (c n) -> p c n", c=2)
        phi_sb, phi_sq = (a.rearrange("p (c n) -> p c n", c=2) for a in (phi_sb, phi_sq))

        psum = ctx.enter_context(nc.psum_tensor("psum", [P, 8, 512], F32))
        PV_BANK, Y_BANK, WO_BANK, SHARED_BANK = 3, 4, 5, 6

        ids_loaded = sem("ids_loaded")
        norm_loaded = sem("norm_loaded")
        wqkv_loaded = sem("wqkv_loaded")
        wo_loaded = sem("wo_loaded")
        phi_loaded = sem("phi_loaded")
        b1_loaded = sem("b1_loaded")
        b2_loaded = sem("b2_loaded")
        consts_ready = sem("consts_ready")
        ids_fixed = sem("ids_fixed")
        ids_turned = sem("ids_turned")
        ids_ready = sem("ids_ready")
        ids_staged = sem("ids_staged")
        gathered = sem("gathered")
        emb_used = sem("emb_used")
        scaled = sem("scaled")
        hidden_ready = sem("hidden_ready")
        xa_ready = sem("xa_ready")
        phi_squared = sem("phi_squared")
        phi_summed = sem("phi_summed")
        phi_ready = sem("phi_ready")
        qk_copied = sem("qk_copied")
        b1_turned = sem("b1_turned")
        b1_ready = sem("b1_ready")
        shared_full = [sem(f"shared_full{i}") for i in range(2)]
        shared_free = [sem(f"shared_free{i}") for i in range(2)]
        diag_ready = sem("diag_ready")
        scores_done = sem("scores_done")
        squared = sem("squared")
        masked = sem("masked")
        pv_done = sem("pv_done")
        pv_copied = sem("pv_copied")
        y_turned = sem("y_turned")
        y_normed = sem("y_normed")
        yn_turned = sem("yn_turned")
        yn_copied = sem("yn_copied")
        wo_done = sem("wo_done")
        attended = sem("attended")
        xn_ready = sem("xn_ready")
        max_d_ready = sem("max_d_ready")
        exp_d_ready = sem("exp_d_ready")
        disp_ready = sem("disp_ready")
        log_c_ready = sem("log_c_ready")
        exp_c_ready = sem("exp_c_ready")
        comb_ready = sem("comb_ready")
        waits_apart = sem("waits_apart")
        zeroed = sem("zeroed")
        vec_step = sem("vec_step")
        w1_loaded = [sem(f"w1_loaded{k}") for k in range(SLOTS)]
        w2_loaded = [sem(f"w2_loaded{k}") for k in range(SLOTS)]
        slots_staged = sem("slots_staged")
        w1_used = sem("w1_used")
        w2_used = sem("w2_used")
        h_copied = sem("h_copied")
        h_turned = sem("h_turned")
        bias_added = sem("bias_added")
        act_ready = sem("act_ready")
        y_low = sem("y_low")
        y_ready = sem("y_ready")
        y_stored = [sem(f"y_stored{i}") for i in range(2)]
        y_loaded = sem("y_loaded")
        combined = sem("combined")
        added = sem("added")
        out_stored = sem("out_stored")

        y_dram = nc.dram_tensor("slot_outputs", [NE * B, D], F32, kind="Internal").ap()

        first_uses, first_seen = shared_uses(PROJECT)
        loop_uses, loop_seen = shared_uses(ORDER)
        last_uses, _ = shared_uses([s for s in ORDER if "'" not in s])

        def shared(stage, q, last):
            if q is None:
                return first_uses[stage]
            bank, before = (last_uses if last else loop_uses)[stage]
            return bank, q * loop_seen[bank] + (first_seen[bank] + before)

        def quads(body):
            def run(eng):
                with eng.Fori(0, NQ - 1) as q:
                    body(q, False)
                body(NQ - 1, True)
            return run

        def first(i):
            return type(i) is int and i == 0

        def groups(eng, group):
            group(0, 0)
            group(0, 1)
            with eng.Fori(1, NG // 2) as i:
                group(i, 0)
                group(i, 1)

        def apart(eng):
            eng.sem_inc(waits_apart, 1)

        def turn(pe, to, of, rows):
            return pe.transpose(to, of, ident[0:rows, 0:rows])

        block = ctx.enter_context(nc.Block())

        @block.sync
        def _(sp):
            raw = ids.bitcast(I32)
            sp.dma_start(raw[0:B, 0:S], x).then_inc(ids_loaded, 16)
            sp.dma_start(raw[0:B, S:2 * S], types).then_inc(ids_loaded, 16)
            sp.dma_start(gam, gamma.rearrange("(o d) -> o d", o=1).to_broadcast([P, D])).then_inc(norm_loaded, 16)
            sp.dma_start(bet, beta.rearrange("(o d) -> o d", o=1).to_broadcast([P, D])).then_inc(norm_loaded, 16)
            for n, w in enumerate((wq, wk, wv)):
                sp.dma_start(w_qkv[0:HD, :, n * D:(n + 1) * D],
                             w.rearrange("(c p) n -> p c n", c=2)).then_inc(wqkv_loaded, 16)
            sp.dma_start(w_o, wo.rearrange("(c p) n -> p c n", c=2)).then_inc(wo_loaded, 16)
            sp.dma_start(phi_sb[0:HD], phi.rearrange("(c p) n o -> p c (n o)", c=2)).then_inc(phi_loaded, 16)
            sp.dma_start(phi_w[0:HD, 3 * NE:3 * NE + 1],
                         scale.rearrange("(o d) -> o d", o=1).to_broadcast([HD, 1])).then_inc(phi_loaded, 16)
            sp.dma_start(b1_sb[0:NE, :], b1).then_inc(b1_loaded, 16)

            w1_pairs = w1.rearrange("(n e) k f -> n (e k) f", e=2).rearrange("n (k p) f -> n p k f", p=P)
            w2_pairs = w2.rearrange("(n e) (p t) d -> n p e t d", e=2, t=KT2)

            def load_group(i, u, first):
                for k in range(GP):
                    slot = GP * u + k
                    if first and slot == EARLY_SLOT:
                        sp.wait_ge(shared_free[last_uses["CT"][0]], last_free)
                    if not first and k == 0:
                        sp.wait_ge(w1_used, 2 * i + (u - 1))
                    sp.dma_start(w1_slot(slot), w1_pairs[bass.ds(i * SLOTS + slot, 1)].squeeze(0)
                                 if not first else w1_pairs[slot]).then_inc(w1_loaded[slot], 16)
                    if first and slot > EARLY_SLOT - 1:
                        continue
                    if first:
                        sp.dma_start(w2_slot(slot), w2_pairs[slot]).then_inc(w2_loaded[slot], 16)
                for k in range(GP):
                    slot = GP * u + k
                    if first and slot < EARLY_SLOT:
                        continue
                    if not first and k == 0:
                        sp.wait_ge(w2_used, 2 * i + (u - 1))
                    sp.dma_start(w2_slot(slot), w2_pairs[bass.ds(i * SLOTS + slot, 1)].squeeze(0)
                                 if not first else w2_pairs[slot]).then_inc(w2_loaded[slot], 16)

            ct_bank, ct_before = shared("CT", NQ - 1, True)
            last_free = ct_before + 1
            sp.wait_ge(gathered, 2 * 16 * 3 * J)
            load_group(0, 0, True)
            load_group(0, 1, True)
            sp.dma_start(slot_out[NE:P], b2.unsqueeze(1).to_broadcast([NE, B, D])).then_inc(b2_loaded, 16)
            with sp.Fori(1, NG // 2) as i:
                load_group(i, 0, False)
                load_group(i, 1, False)
            for i in range(2):
                sp.wait_ge(y_stored[i], 16 * (NG // 2))
            sp.dma_start(slot_out[0:NE], y_dram.rearrange("(n b) d -> n b d", b=B)).then_inc(y_loaded, 16)
            for c in range(NQ):
                sp.wait_ge(added, J * (c + 1))
                sp.dma_start(out[J * c:J * (c + 1)].rearrange("b m d -> m b d"),
                             hidden[:, J * c:J * (c + 1), :]).then_inc(out_stored, 16)
            sp.wait_ge(out_stored, 16 * NQ)

        @block.gpsimd
        def _(pool):
            pool.memset(ident, 0.0).then_inc(zeroed, 1)
            pool.memset(mask, 1.0).then_inc(zeroed, 1)
            pool.memset(head_mask[0:HD, :], 1.0).then_inc(zeroed, 1)
            pool.memset(ones[0:HD, :], 1.0).then_inc(consts_ready, 1)
            pool.wait_ge(zeroed, 3)
            pool.affine_select(out=ident, in_=ident, compare_op=ALU.not_equal, fill=1.0, base=0,
                               pattern=[[-1, P]], channel_multiplier=1).then_inc(consts_ready, 1)
            pool.affine_select(out=mask, in_=mask, compare_op=ALU.is_ge, fill=0.0, base=0,
                               pattern=[[1, S]], channel_multiplier=-1).then_inc(consts_ready, 1)
            pool.affine_select(out=head_mask[0:HD, :], in_=head_mask[0:HD, :], compare_op=ALU.is_ge, fill=0.0,
                               base=0, pattern=[[-FD, HH]], channel_multiplier=1).then_inc(zeroed, 1)
            pool.wait_ge(zeroed, 4)
            pool.affine_select(out=head_mask[0:HD, :], in_=head_mask[0:HD, :], compare_op=ALU.is_ge, fill=0.0,
                               base=FD - 1, pattern=[[FD, HH]], channel_multiplier=-1).then_inc(consts_ready, 1)
            pool.iota(odd, pattern=[[0, 1]], base=0, channel_multiplier=1).then_inc(consts_ready, 1)
            pool.memset(v_aug[:, :, :, FD:32], 1.0).then_inc(consts_ready, 1)
            pool.memset(slots_t, 0.0).then_inc(consts_ready, 1)

            pool.wait_ge(norm_loaded, 32)
            pool.wait_ge(ids_ready, 1)
            id_all = small[:, 0:3 * B].bitcast(U32).rearrange("p (t b) -> p t b", t=3)
            id_quad = small[:, 48:48 + 3 * J].bitcast(U32).rearrange("p (t j) -> p t j", t=3)

            def embed(q):
                pool.tensor_copy(id_quad, id_all[:, :, bass.ds(q * J, J)]).then_inc(ids_staged, 1)
                pool.wait_ge(ids_staged, q + 1)
                apart(pool)
                for t, table in enumerate((tok_table, pos_table, type_table)):
                    for j in range(J):
                        pool.indirect_dma_start(
                            out=emb[:, t, j, :], out_offset=None, in_=table,
                            in_offset=bass.IndirectOffsetOnAxis(ap=id_quad[:, t, j:j + 1], axis=0),
                        ).then_inc(gathered, 16)
                part = hidden[:, bass.ds(q * J, J), :]
                pool.wait_ge(emb_used, q + 1)
                pool.tensor_tensor(part, part, gam.unsqueeze(1).to_broadcast([P, J, D]), ALU.mult)\
                    .then_inc(scaled, 1)
                pool.wait_ge(scaled, q + 1)
                apart(pool)
                pool.tensor_tensor(part, part, bet.unsqueeze(1).to_broadcast([P, J, D]), ALU.add)\
                    .then_inc(hidden_ready, 1)

            with pool.Fori(0, NQ) as q:
                embed(q)

            xs_bank, xs_before = shared("XS", NQ - 1, True)
            pool.wait_ge(shared_free[xs_bank], xs_before + 1)
            ct_bank, ct_before = shared("CT", NQ - 1, True)
            pool.wait_ge(shared_free[ct_bank], ct_before + 1)

            def stage(i, u):
                if not first(i):
                    pool.wait_ge(w1_used, 2 * i + (u - 1))
                pool.tensor_copy(staged[u], slots_t[:, :, bass.ds(i * SLOTS + GP * u, GP), :])\
                    .then_inc(slots_staged, 1)

            groups(pool, stage)

        @block.tensor
        def _(pe):
            pe.wait_ge(consts_ready, 7)

            def project(stage, q, quad, last):
                bank, before = shared(stage + ("'" if q is not None else ""), q, last)
                to = psum[:, SHARED_BANK + bank, :]
                if q is not None or before > 0:
                    pe.wait_ge(shared_free[bank], before)
                if stage == "XT0":
                    pe.wait_ge(xa_ready, quad + 1)
                if stage[:2] == "XT":
                    c = int(stage[2])
                    for j in range(J):
                        mm = turn(pe, to[0:HD, j * S:(j + 1) * S], xa[:, j, c * HD:(c + 1) * HD], P)
                elif stage[:2] == "QK":
                    n = int(stage[2])
                    if n == 0:
                        wait_shared_free("XT0", q, last)
                        wait_shared_free("XT1", q, last)
                    for c in range(2):
                        mm = pe.matmul(to[0:HD, :], w_qkv[0:HD, c, n * HD:(n + 1) * HD], xa_t[0:HD, c, :],
                                       start=(c == 0), stop=(c == 1))
                else:
                    for r in range(2):
                        j = 2 * int(stage[1]) + r
                        for c in range(2):
                            mm = pe.matmul(to[:, r * D:(r + 1) * D], xa_t[0:HD, c, j * S:(j + 1) * S],
                                           w_qkv[0:HD, c, 2 * D:3 * D], start=(c == 0), stop=(c == 1))
                mm.then_inc(shared_full[bank], 1)

            def wait_shared_free(stage, q, last):
                bank, before = shared(stage + ("'" if q is not None else ""), q, last)
                pe.wait_ge(shared_free[bank], before + 1)

            def scores(q, j):
                b = q * J + j
                if j == 0:
                    pe.wait_ge(qk_copied, 4 * (q + 1))
                for m, (bank, g, h0, n) in enumerate([(0, 0, 0, 4), (1, 0, 4, 2), (1, 1, 0, 2), (2, 1, 2, 4)]):
                    pe.wait_ge(diag_ready, 2 * b + (g + 1))
                    if j > 0 and m != 2:
                        pe.wait_ge(squared, 3 * b + (bank - 2))
                    at = {0: 0, 1: 0, 2: 2 * S, 3: 0}[m]
                    pe.matmul(psum[:, bank, at:at + n * S], k_t[0:HD, g, j * S:(j + 1) * S],
                              q_diag[0:HD, g, h0:h0 + n, :], start=True, stop=True,
                              skip_group_check=True).then_inc(scores_done, 1)

            def weigh(q, j):
                b = q * J + j
                if j > 0:
                    pe.wait_ge(pv_copied, b)
                for h in range(H):
                    if h % 4 == 0:
                        pe.wait_ge(masked, 3 * b + (h // 4 + 1))
                    c = 32 * (h % 4)
                    mm = pe.matmul(psum[c:c + 32, PV_BANK, (h // 4) * S:(h // 4 + 1) * S], v_aug[:, j, h, :],
                                   probs[:, j % 2, h, :], start=True, stop=True, skip_group_check=True)
                mm.then_inc(pv_done, 1)

            def turn_y(q, j):
                b = q * J + j
                pe.wait_ge(pv_copied, b + 1)
                if j > 0:
                    pe.wait_ge(yn_copied, b)
                for k in range(3):
                    mm = turn(pe, psum[:, Y_BANK, k * S:(k + 1) * S], pv_sb[:, k * S:(k + 1) * S], P)
                mm.then_inc(y_turned, 1)

            def turn_yn(q, j):
                b = q * J + j
                pe.wait_ge(y_normed, b + 1)
                for c in range(2):
                    mm = turn(pe, psum[0:HD, Y_BANK, c * S:(c + 1) * S], yn[:, c * HD:(c + 1) * HD], P)
                mm.then_inc(yn_turned, 1)

            def project_out(q, j):
                b = q * J + j
                pe.wait_ge(yn_copied, b + 1)
                if j > 0:
                    pe.wait_ge(attended, b)
                for c in range(2):
                    mm = pe.matmul(psum[:, WO_BANK, 0:D], yn_t[0:HD, c, :], w_o[:, c, :],
                                   start=(c == 0), stop=(c == 1))
                mm.then_inc(wo_done, 1)

            def route(stage, q, last):
                bank, before = shared(stage, q, last)
                to = psum[:, SHARED_BANK + bank, :]
                pe.wait_ge(shared_free[bank], before)
                if stage in ("XN0", "XN1"):
                    c = int(stage[2])
                    pe.wait_ge(xn_ready, q + 1)
                    for j in range(J):
                        mm = turn(pe, to[0:HD, j * S:(j + 1) * S], xn[:, j, c * HD:(c + 1) * HD], P)
                elif stage == "LT":
                    for s in ("XN0", "XN1"):
                        n, k = shared(s, q, last)
                        pe.wait_ge(shared_free[n], k + 1)
                    for j in range(J):
                        r, i = j % 2, j // 2
                        for c in range(2):
                            mm = pe.matmul(to[NE * r:NE * (r + 1), i * S:(i + 1) * S], phi_n2[0:HD, c, :],
                                           xn_t[0:HD, c, j * S:(j + 1) * S], start=(c == 0), stop=(c == 1),
                                           skip_group_check=True)
                elif stage == "LN":
                    n, k = shared("LT", q, last)
                    pe.wait_ge(shared_free[n], k + 1)
                    for i in range(2):
                        mm = turn(pe, to[:, i * P:(i + 1) * P], log_t[:, i, :], P)
                elif stage == "DT":
                    pe.wait_ge(disp_ready, q + 1)
                    for i in range(2):
                        mm = turn(pe, to[:, i * P:(i + 1) * P], disp[:, i, :], P)
                elif stage == "XS":
                    n, k = shared("DT", q, last)
                    pe.wait_ge(shared_free[n], k + 1)
                    for j in range(J):
                        even, oddn = disp_t[:, j, 0:NE:2], disp_t[:, j, 1:NE:2]
                        at = j * NPAIR
                        for rows, tile, lo, hi, rhs in ((slice(0, P), 0, 0, P, even), (slice(0, P), 1, D - P, D, oddn),
                                                        (slice(0, NE), 2, P, D, even), (slice(NE, P), 2, 0, D - P, oddn)):
                            mm = pe.matmul(to[rows, tile * P + at:tile * P + at + NPAIR], xn[:, j, lo:hi], rhs,
                                           start=True, stop=True, skip_group_check=True)
                else:
                    pe.wait_ge(comb_ready, q + 1)
                    for j in range(J):
                        mm = turn(pe, to[:, j * S:(j + 1) * S], comb[:, j].rearrange("p r n -> p (r n)"), P)
                mm.then_inc(shared_full[bank], 1)

            def body(q, last):
                for stage in ORDER:
                    if "'" in stage:
                        if not last:
                            project(stage[:-1], q, q + 1, last)
                    elif stage[:2] in stages:
                        stages[stage[:2]](q, int(stage[2]))
                    elif stage[0] == "S" and stage[1] in "0123":
                        scores(q, int(stage[1]))
                    else:
                        route(stage, q, last)

            stages = {"PV": weigh, "YT": turn_y, "YN": turn_yn, "WO": project_out}

            pe.wait_ge(ids_fixed, 1)
            for t in range(3):
                mm = turn(pe, psum[:, Y_BANK, t * B:(t + 1) * B], ids_f[0:B, t, :], B)
            mm.then_inc(ids_turned, 1)
            pe.wait_ge(phi_squared, 1)
            for c in range(2):
                mm = pe.matmul(psum[0:HD, WO_BANK, 0:NE], ones[0:HD, :], phi_sq[0:HD, c, :],
                               start=(c == 0), stop=(c == 1))
            mm.then_inc(phi_summed, 1)
            pe.wait_ge(b1_loaded, 16)
            for t in range(KT2):
                mm = turn(pe, psum[:, PV_BANK, t * NE:(t + 1) * NE], b1_sb[0:NE, t:F:KT2], NE)
            mm.then_inc(b1_turned, 1)

            pe.wait_ge(wqkv_loaded, 48)
            for stage in PROJECT:
                project(stage, None, 0, False)
            pe.wait_ge(wo_loaded, 16)
            pe.wait_ge(phi_ready, 1)
            pe.wait_ge(b1_ready, 1)
            quads(body)(pe)

            def group(i, u):
                g = 2 * i + u
                pe.wait_ge(slots_staged, g + 1)
                for k in range(GP):
                    pe.wait_ge(w1_loaded[GP * u + k], 16 * (i + 1))
                for kt in range(KT1):
                    for half in range(2):
                        for k in range(GP):
                            mm = pe.matmul(psum[32 * k:32 * k + 32, half, 0:F // 2], staged[u][:, kt, k, :],
                                           w1_slot(GP * u + k)[:, kt, half * (F // 2):(half + 1) * (F // 2)],
                                           start=(kt == 0), stop=(kt == KT1 - 1), skip_group_check=True)
                mm.then_inc(w1_used, 1)
                pe.wait_ge(h_copied, 2 * g + 2)
                for t in range(KT2):
                    mm = turn(pe, psum[:, 2 + t // 4, (t % 4) * P:(t % 4 + 1) * P], h_sb[:, t, :], P)
                    if t in (3, KT2 - 1):
                        mm.then_inc(h_turned, 1)
                for k in range(GP):
                    pe.wait_ge(w2_loaded[GP * u + k], 16 * (i + 1))
                if u or not first(i):
                    pe.wait_ge(y_ready, g)
                for t in range(KT2):
                    if t in (0, 4):
                        pe.wait_ge(act_ready, 2 * g + (1 if t == 0 else 2))
                    for k in range(GP):
                        mm = pe.matmul(psum[32 * k:32 * k + 32, 4, 0:2 * D], act_t[:, t, 32 * k:32 * k + 32],
                                       w2_slot(GP * u + k)[:, :, t, :], start=(t == 0), stop=(t == KT2 - 1),
                                       skip_group_check=True)
                mm.then_inc(w2_used, 1)

            groups(pe, group)

            pe.wait_ge(b2_loaded, 16)
            pe.wait_ge(y_loaded, 16)
            for b in range(B):
                if b >= 8:
                    pe.wait_ge(added, b - 7)
                pe.matmul(psum[:, b % 8, 0:D], combine_t[:, b, :], slot_out[:, b, :],
                          start=True, stop=True).then_inc(combined, 1)

        @block.vector
        def _(dve):
            STEPS = {"first": 59, "quad": 64}
            base, done = [0], [0]

            def step(ins):
                done[0] += 1
                ins.then_inc(vec_step, 1)
                dve.wait_ge(vec_step, base[0] + done[0])

            def rsqrt(y, v, t):
                step(dve.tensor_scalar(y.bitcast(I32), v.bitcast(I32), 1, None, ALU.logical_shift_right))
                step(dve.tensor_scalar(y.bitcast(I32), y.bitcast(I32), -1.0, MAGIC, ALU.mult, ALU.add))
                for _ in range(3):
                    step(dve.scalar_tensor_tensor(out=t, in0=v, scalar=-0.5, in1=y, op0=ALU.mult, op1=ALU.mult))
                    step(dve.tensor_tensor(t, t, y, ALU.mult))
                    step(dve.scalar_tensor_tensor(out=y, in0=t, scalar=1.5, in1=y, op0=ALU.add, op1=ALU.mult))

            stats = small[:, 60:84].rearrange("p (j s) -> p j s", j=J)
            mv = small[:, 84:92].rearrange("p (j s) -> p j s", j=J)
            vs = small[:, 92:100].rearrange("p (s j) -> p s j", s=2)
            rs = small[:, 100:108].rearrange("p (s j) -> p s j", s=2)
            tmp = small[:, 108:116].rearrange("p (s j) -> p s j", s=2)
            max_d, den_d, rec_d = small[:, 116:118], small[:, 118:120], small[:, 120:122]
            max_c, den_c, rec_c = small[:, 122:126], small[:, 126:130], small[:, 130:134]
            den_y, rec_y = small[:, 134:146], small[:, 146:158]

            def moments(rows):
                apart(dve)
                for j in range(J):
                    ins = dve.bn_stats(stats[:, j, :], rows(j))
                step(ins)
                apart(dve)
                for j in range(J):
                    ins = dve.bn_aggr(mv[:, j, :], stats[:, j, :])
                step(ins)

            def embed_norm(q):
                dve.wait_ge(gathered, 192 * (q + 1))
                step(dve.tensor_tensor(emb[:, 0], emb[:, 0], emb[:, 1], ALU.add))
                step(dve.tensor_tensor(emb[:, 0], emb[:, 0], emb[:, 2], ALU.add))
                moments(lambda j: emb[:, 0, j, :])
                step(dve.tensor_scalar(vs[:, 0, :], mv[:, :, 1], 1e-12, None, ALU.add))
                rsqrt(rs[:, 0, :], vs[:, 0, :], tmp[:, 0, :])
                for j in range(J):
                    ins = dve.tensor_scalar(hidden[:, bass.ds(q * J + j, 1), :], emb[:, 0, j:j + 1, :],
                                            mv[:, j, 0:1], rs[:, 0, j:j + 1], ALU.subtract, ALU.mult)
                ins.then_inc(emb_used, 1)

            def attn_norm(q):
                dve.wait_ge(hidden_ready, q + 1)
                moments(lambda j: hidden[:, bass.ds(q * J + j, 1), :])
                step(dve.tensor_scalar(vs[:, 0, :], mv[:, :, 1], 1e-5, None, ALU.add))
                rsqrt(rs[:, 0, :], vs[:, 0, :], tmp[:, 0, :])
                for j in range(J):
                    ins = dve.tensor_scalar(xa[:, j:j + 1, :], hidden[:, bass.ds(q * J + j, 1), :],
                                            mv[:, j, 0:1], rs[:, 0, j:j + 1], ALU.subtract, ALU.mult)
                ins.then_inc(xa_ready, 1)

            def diagonal(q, j):
                b = q * J + j
                if j == 0:
                    dve.wait_ge(qk_copied, 4 * q + 2)
                for g in range(2):
                    if j > 0:
                        dve.wait_ge(scores_done, 4 * b - 2 + 2 * g)
                    dve.tensor_tensor(
                        q_diag[0:HD, g], q_t[0:HD, g, j * S:(j + 1) * S].unsqueeze(1).to_broadcast([HD, HH, S]),
                        head_mask[0:HD, :].unsqueeze(2).to_broadcast([HD, HH, S]), ALU.mult).then_inc(diag_ready, 1)

            def mask_scores(q, j):
                b = q * J + j
                for k in range(3):
                    part = probs[:, j % 2, 4 * k:4 * k + 4, :]
                    dve.wait_ge(squared, 3 * b + (k + 1))
                    dve.scalar_tensor_tensor(out=part, in0=part, scalar=1.0,
                                             in1=mask.unsqueeze(1).to_broadcast([P, 4, S]),
                                             op0=ALU.add, op1=ALU.mult).then_inc(masked, 1)

            def normalise_y(q, j):
                b = q * J + j
                dve.wait_ge(y_turned, b + 1)
                heads = psum[:, Y_BANK, 0:3 * S].rearrange("p (h e) -> p h e", e=32)
                step(dve.tensor_scalar(den_y, heads[:, :, FD], 2e-12, None, ALU.add))
                step(dve.reciprocal(rec_y, den_y))
                dve.tensor_tensor(yn.rearrange("p (h e) -> p h e", e=FD), heads[:, :, 0:FD],
                                  rec_y.unsqueeze(2).to_broadcast([P, H, FD]), ALU.mult).then_inc(y_normed, 1)

            def add_attention(q, j):
                b = q * J + j
                dve.wait_ge(wo_done, b + 1)
                row = hidden[:, bass.ds(b, 1), :]
                dve.tensor_tensor(row, row, psum[:, WO_BANK, 0:D].unsqueeze(1), ALU.add).then_inc(attended, 1)

            def route_norm(q):
                dve.wait_ge(attended, J * (q + 1))
                moments(lambda j: hidden[:, bass.ds(q * J + j, 1), :])
                step(dve.tensor_scalar(vs[:, 0, :], mv[:, :, 1], 1e-5, None, ALU.add))
                step(dve.tensor_scalar(vs[:, 1, :], mv[:, :, 1], float(D), None, ALU.mult))
                rsqrt(rs, vs, tmp)
                step(dve.tensor_tensor(tmp[:, 0, :], vs[:, 1, :], rs[:, 1, :], ALU.mult))
                step(dve.tensor_tensor(tmp[:, 0, :], tmp[:, 0, :], rs[:, 0, :], ALU.mult))
                step(dve.tensor_scalar(tmp[:, 0, :], tmp[:, 0, :], 1e-12, None, ALU.max))
                step(dve.reciprocal(tmp[:, 1, :], tmp[:, 0, :]))
                step(dve.tensor_tensor(rs[:, 1, :], rs[:, 0, :], tmp[:, 1, :], ALU.mult))
                for j in range(J):
                    ins = dve.tensor_scalar(xn[:, j:j + 1, :], hidden[:, bass.ds(q * J + j, 1), :],
                                            mv[:, j, 0:1], rs[:, 1, j:j + 1], ALU.subtract, ALU.mult)
                ins.then_inc(xn_ready, 1)

            def dispatch_max(q, last):
                bank, before = shared("LT", q, last)
                dve.wait_ge(shared_full[bank], before + 1)
                dve.tensor_reduce(max_d, psum[:, SHARED_BANK + bank, 0:256].rearrange("p (i m) -> p i m", i=2),
                                  AX.X, ALU.max, negate=True).then_inc(max_d_ready, 1)

            def dispatch_norm(q):
                dve.wait_ge(exp_d_ready, 2 * (q + 1))
                step(dve.reciprocal(rec_d, den_d))
                for i in range(2):
                    ins = dve.tensor_scalar(disp[:, i, :], exp_d[:, i, :], rec_d[:, i:i + 1], None, ALU.mult)
                ins.then_inc(disp_ready, 1)

            def combine_max(q, last):
                bank, before = shared("LN", q, last)
                dve.wait_ge(shared_full[bank], before + 1)
                logits = psum[:, SHARED_BANK + bank, 0:256].rearrange("p (j n) -> p j n", j=J)
                step(dve.tensor_reduce(max_c, logits, AX.X, ALU.max))
                step(dve.tensor_tensor(log_c, logits, max_c.unsqueeze(2).to_broadcast([P, J, NE]), ALU.subtract))
                dve.sem_inc(shared_free[bank], 1)
                dve.sem_inc(log_c_ready, 1)

            def combine_norm(q):
                dve.wait_ge(exp_c_ready, q + 1)
                step(dve.tensor_reduce(den_c, exp_c, AX.X, ALU.add))
                step(dve.reciprocal(rec_c, den_c))
                step(dve.tensor_tensor(exp_c, exp_c, rec_c.unsqueeze(2).to_broadcast([P, J, NE]), ALU.mult))
                dve.tensor_copy(comb, exp_c.unsqueeze(2).to_broadcast([P, J, 2, NE])).then_inc(comb_ready, 1)

            def body(q, last):
                base[0], done[0] = STEPS["quad"] * q + STEPS["first"], 0
                diagonal(q, 1)
                mask_scores(q, 0)
                diagonal(q, 2)
                mask_scores(q, 1)
                normalise_y(q, 0)
                diagonal(q, 3)
                mask_scores(q, 2)
                if not last:
                    embed_norm(q + 1)
                add_attention(q, 0)
                normalise_y(q, 1)
                mask_scores(q, 3)
                if not last:
                    attn_norm(q + 1)
                add_attention(q, 1)
                normalise_y(q, 2)
                add_attention(q, 2)
                normalise_y(q, 3)
                add_attention(q, 3)
                route_norm(q)
                if not last:
                    diagonal(q + 1, 0)
                dispatch_max(q, last)
                dispatch_norm(q)
                combine_max(q, last)
                combine_norm(q)
                if not last:
                    assert done[0] == STEPS["quad"], done[0]

            dve.wait_ge(ids_loaded, 32)
            raw = ids.bitcast(I32)
            step(dve.tensor_copy(ids_f[0:B, 0, :], raw[0:B, 0:S]))
            step(dve.tensor_copy(ids_f[0:B, 2, :], raw[0:B, S:2 * S]))
            step(dve.tensor_copy(ids_f[0:B, 1, :], ids_f[0:B, 0, :]))
            for t, n in enumerate(TABLES):
                f = ids_f[0:B, t, :]
                step(dve.tensor_scalar(ids_w[0:B, :], f, 0.0, float(n), ALU.is_lt, ALU.mult))
                step(dve.tensor_tensor(f, f, ids_w[0:B, :], ALU.add))
                step(dve.tensor_scalar(f, f, 0.0, float(n - 1), ALU.max, ALU.min))
            dve.sem_inc(ids_fixed, 1)
            dve.wait_ge(ids_turned, 1)
            dve.tensor_copy(small[:, 0:3 * B].bitcast(U32), psum[:, Y_BANK, 0:3 * B]).then_inc(ids_ready, 1)
            dve.wait_ge(consts_ready, 7)
            step(dve.tensor_scalar(odd, odd, 4, 1, ALU.logical_shift_right, ALU.bitwise_and))

            dve.wait_ge(phi_loaded, 32)
            dve.tensor_tensor(phi_sq[0:HD], phi_sb[0:HD], phi_sb[0:HD], ALU.mult).then_inc(phi_squared, 1)
            dve.wait_ge(phi_summed, 1)
            n2, r, t = (phi_w[0:HD, i * NE:(i + 1) * NE] for i in range(3))
            step(dve.tensor_copy(n2, psum[0:HD, WO_BANK, 0:NE]))
            rsqrt(r, n2, t)
            step(dve.tensor_tensor(t, n2, r, ALU.mult))
            step(dve.tensor_scalar(t, t, 1e-12, None, ALU.max))
            step(dve.reciprocal(r, t))
            step(dve.tensor_scalar(r, r, phi_w[0:HD, 3 * NE:3 * NE + 1], None, ALU.mult))
            dve.tensor_tensor(phi_n2[0:HD], phi_sb[0:HD], r.unsqueeze(1).to_broadcast([HD, 2, NE]), ALU.mult)\
                .then_inc(phi_ready, 1)
            dve.wait_ge(b1_turned, 1)
            dve.tensor_copy(b1_t, psum[:, PV_BANK, 0:KT2 * NE].rearrange("p (t n) -> p t n", t=KT2))\
                .then_inc(b1_ready, 1)

            embed_norm(0)
            attn_norm(0)
            diagonal(0, 0)
            assert done[0] == STEPS["first"], done[0]
            quads(body)(dve)

            def group(i, u):
                g = 2 * i + u
                dve.wait_ge(w1_used, g + 1)
                dve.tensor_copy(h_sb[:, :, P // 2:P].rearrange("p t c -> p c t"),
                                psum[:, 1, 0:F // 2].rearrange("p (c t) -> p c t", t=KT2)).then_inc(h_copied, 1)
                for part, (t0, t1) in enumerate(((0, 4), (4, KT2))):
                    dve.wait_ge(h_turned, 2 * g + (part + 1))
                    dve.tensor_tensor(
                        h_t[:, t0:t1], psum[:, 2 + part, 0:(t1 - t0) * P].rearrange("p (t e b) -> p t e b", e=G, b=B),
                        b1_t[:, t0:t1, bass.ds(g * G, G)].unsqueeze(3).to_broadcast([P, t1 - t0, G, B]),
                        ALU.add).then_inc(bias_added, 1)
                dve.wait_ge(y_low, g + 1)
                apart(dve)
                dve.copy_predicated(y_sb[u], odd.to_broadcast([P, D]), psum[:, 4, D:2 * D]).then_inc(y_ready, 1)

            dve.wait_ge(slots_staged, 1)
            groups(dve, group)

            for b in range(B):
                dve.wait_ge(combined, b + 1)
                dve.tensor_tensor(hidden[:, b, :], hidden[:, b, :], psum[:, b % 8, 0:D], ALU.add)\
                    .then_inc(added, 1)

        @block.scalar
        def _(act):
            def evacuate(stage, q, last):
                bank, before = shared(stage, q, last)
                full = psum[:, SHARED_BANK + bank, :]
                act.wait_ge(shared_full[bank], before + 1)
                name = stage.rstrip("'")
                if name[:2] == "XT":
                    ins = act.copy(xa_t[0:HD, int(name[2]), :], full[0:HD, :])
                elif name[:2] == "QK":
                    n = int(name[2])
                    act.copy((q_t if n < 2 else k_t)[0:HD, n % 2, :], full[0:HD, :]).then_inc(qk_copied, 1)
                    act.wait_ge(qk_copied, 4 * (0 if q is None else q + 1) + (n + 1))
                    act.sem_inc(shared_free[bank], 1)
                    return
                elif name in ("V0", "V1"):
                    r = 2 * int(name[1])
                    ins = act.copy(v_aug[:, r:r + 2, :, 0:FD],
                                   full[:, 0:2 * D].rearrange("p (r h e) -> p r h e", r=2, e=FD))
                elif name[:2] == "XN":
                    ins = act.copy(xn_t[0:HD, int(name[2]), :], full[0:HD, :])
                elif name == "DT":
                    ins = act.copy(disp_t, full[:, 0:256].rearrange("p (j n) -> p j n", j=J))
                elif name == "XS":
                    part = full[:, 0:3 * P].rearrange("p (t j n) -> p t n j", t=3, j=J)
                    act.copy(slots_t[:, 0, :, bass.ds(q * J, J)], part[:, 0])
                    act.copy(slots_t[:, 2, :, bass.ds(q * J + B, J)], part[:, 1])
                    act.copy(slots_t[0:NE, 1, :, bass.ds(q * J, J)], part[0:NE, 2])
                    ins = act.copy(slots_t[NE:P, 1, :, bass.ds(q * J + B, J)], part[NE:P, 2])
                elif name == "CT":
                    ins = act.copy(combine_t[:, bass.ds(q * J, J), :], full.rearrange("p (j m) -> p j m", j=J))
                ins.then_inc(shared_free[bank], 1)

            def square(q, j):
                b = q * J + j
                for k, ready in enumerate((1, 3, 4)):
                    act.wait_ge(scores_done, 4 * b + ready)
                    act.activation(probs[:, j % 2, 4 * k:4 * k + 4, :],
                                   psum[:, k, :].rearrange("p (h m) -> p h m", h=4), ACT.Square,
                                   bias=1.0, scale=0.25).then_inc(squared, 1)

            def copy_pv(q, j):
                act.wait_ge(pv_done, q * J + (j + 1))
                act.copy(pv_sb, psum[:, PV_BANK, 0:3 * S]).then_inc(pv_copied, 1)

            def copy_yn(q, j):
                act.wait_ge(yn_turned, q * J + (j + 1))
                act.copy(yn_t[0:HD], psum[0:HD, Y_BANK, 0:2 * S].rearrange("p (c m) -> p c m", c=2))\
                    .then_inc(yn_copied, 1)

            def dispatch_exp(q, last):
                bank, before = shared("LT", q, last)
                logits = psum[:, SHARED_BANK + bank, 0:256].rearrange("p (i m) -> p i m", i=2)
                act.wait_ge(max_d_ready, q + 1)
                for i in range(2):
                    act.activation(exp_d[:, i, :], logits[:, i, :], ACT.Exp, bias=small[:, 116 + i:117 + i],
                                   accum_out=small[:, 118 + i:119 + i]).then_inc(exp_d_ready, 1)
                act.copy(log_t, logits).then_inc(shared_free[bank], 1)

            def combine_exp(q):
                act.wait_ge(log_c_ready, q + 1)
                act.activation(exp_c, log_c, ACT.Exp).then_inc(exp_c_ready, 1)

            def body(q, last):
                def nxt(*stages):
                    if not last:
                        for s in stages:
                            evacuate(s + "'", q, last)
                square(q, 0)
                square(q, 1)
                copy_pv(q, 0)
                square(q, 2)
                copy_pv(q, 1)
                copy_yn(q, 0)
                square(q, 3)
                copy_pv(q, 2)
                copy_yn(q, 1)
                nxt("XT0", "XT1")
                copy_pv(q, 3)
                copy_yn(q, 2)
                nxt("QK0", "QK1")
                copy_yn(q, 3)
                nxt("QK2", "QK3")
                evacuate("XN0", q, last)
                evacuate("XN1", q, last)
                nxt("V0")
                dispatch_exp(q, last)
                nxt("V1")
                evacuate("DT", q, last)
                combine_exp(q)
                evacuate("XS", q, last)
                evacuate("CT", q, last)

            act.wait_ge(consts_ready, 7)
            for stage in PROJECT:
                evacuate(stage, None, False)
            quads(body)(act)

            def group(i, u):
                g = 2 * i + u
                act.wait_ge(w1_used, g + 1)
                act.copy(h_sb[:, :, 0:P // 2].rearrange("p t c -> p c t"),
                         psum[:, 0, 0:F // 2].rearrange("p (c t) -> p c t", t=KT2)).then_inc(h_copied, 1)
                for part, (t0, t1) in enumerate(((0, 4), (4, KT2))):
                    act.wait_ge(bias_added, 2 * g + (part + 1))
                    act.activation(act_t[:, t0:t1, :], h_t[:, t0:t1].rearrange("p t e b -> p t (e b)"), ACT.Gelu)\
                        .then_inc(act_ready, 1)
                act.wait_ge(w2_used, g + 1)
                if not first(i):
                    act.wait_ge(y_stored[u], 16 * i)
                act.copy(y_sb[u], psum[:, 4, 0:D]).then_inc(y_low, 1)
                act.wait_ge(y_ready, g + 1)
                act.dma_start(y_dram[bass.ds(g * P, P), :], y_sb[u]).then_inc(y_stored[u], 16)

            groups(act, group)


_INS = ['x', 'mask_BS_i1_0', 'L0_tok_tok_table', 'L0_tok_pos_table', 'L0_tok_type_table', 'L0_tok_gamma',
        'L0_tok_beta', 'L0_attn_Wq', 'L0_attn_Wk', 'L0_attn_Wv', 'L0_attn_Wo', 'L0_ffn_phi', 'L0_ffn_scale',
        'L0_ffn_w1', 'L0_ffn_b1', 'L0_ffn_w2', 'L0_ffn_b2']
_OUT = ((16, 128, 192), 'float32')


def kernel(**inputs):
    import numpy as _np
    import concourse.bacc as _bacc
    from concourse import mybir as _mybir
    from concourse.bass_utils import run_bass_kernel_spmd as _run

    nc = _bacc.Bacc("TRN2", target_bir_lowering=False, num_devices=1)
    arrays, args = {}, []
    for name in _INS:
        a = _np.ascontiguousarray(inputs[name])
        arrays[f"in_{name}_dram"] = a
        args.append(nc.dram_tensor(f"in_{name}_dram", a.shape, _mybir.dt.from_np(a.dtype), kind="ExternalInput").ap())
    shape, dtype = _OUT
    args.append(nc.dram_tensor("out_0_dram", shape, _mybir.dt.from_np(_np.dtype(dtype)), kind="ExternalOutput").ap())
    tower_kernel(nc, *args)
    r = _run(nc, [arrays], core_ids=[0])
    return r.results[0]["out_0_dram"]
```

```python
from contextlib import ExitStack

import concourse.bass as bass
from concourse import mybir

F32 = mybir.dt.float32
I32 = mybir.dt.int32
U32 = mybir.dt.uint32
ACT = mybir.ActivationFunctionType
ALU = mybir.AluOpType
AX = mybir.AxisListType

P = 128
B, S = 16, 128
D = 192
HD = D // 2
H, FD = 12, 16
HH = H // 2
NE, F = 64, 768
NC, J = 8, 2
NPAIR = NE // 2
G = 8
NG = NE // G
GP = G // 2
KT1 = 2 * D // P
KT2 = F // P
SLOTS = 2 * GP
W1C = KT1 * F
W2C = 2 * KT2 * D
SLOT = W1C + W2C
LATE = 7620
TABLES = (8000, 128, 2)
MAGIC = float(0x5F3759DF)

PROJECT = ["XT'", "QK0'", "QK1'", "V'"]
ORDER = ["S0", "S1", "PV0", "XN~", "YT0", "LT~", "PV1", "YN0", "XT'", "LN~", "WO0", "YT1", "QK0'", "DT~", "YN1",
         "XS~", "WO1", "QK1'", "CT~", "V'"]


def shared_uses(order):
    marked = [s for s in order if s[-1] in "'~"]
    return {s: (n % 2, n // 2) for n, s in enumerate(marked)}


def tower_kernel(nc, x, types, tok_table, pos_table, type_table, gamma, beta, wq, wk, wv, wo, phi, scale,
                 w1, b1, w2, b2, out):
    with ExitStack() as ctx:
        def sb(name, cols, parts=P):
            return ctx.enter_context(nc.sbuf_tensor(name, [parts, cols], F32))

        def sem(name):
            return ctx.enter_context(nc.semaphore(name))

        ring = sb("ring", SLOTS * SLOT)
        hidden = sb("hidden", B * D)[:, :].rearrange("p (b d) -> p b d", b=B)
        slots_t = sb("slots_t", KT1 * NPAIR * 32)[:, :].rearrange("p (k n c) -> p k n c", k=KT1, n=NPAIR)
        combine_t = sb("combine_t", B * S)[:, :].rearrange("p (b m) -> p b m", b=B)
        ident = sb("ident", P)[:, :]
        b1_t = sb("b1_t", KT2 * NE)[:, :].rearrange("p (t n) -> p t n", t=KT2)
        odd = sb("odd", 1)[:, :].bitcast(I32)
        late = sb("late", LATE)

        def carve(tensor, at, sizes):
            views = []
            for n in sizes:
                views.append(tensor[:, at:at + n])
                at += n
            return views, at

        (slot_out, h_sb, h_t, act_t, staged0, staged1, y_sb0, y_sb1), end = carve(
            late, 0, [B * D, F, F, F, KT1 * GP * 32, KT1 * GP * 32, D, D])
        assert end <= LATE
        slot_out = slot_out.rearrange("p (b d) -> p b d", b=B)
        h_sb = h_sb.rearrange("p (t c) -> p t c", t=KT2)
        h_t = h_t.rearrange("p (t e b) -> p t e b", t=KT2, e=G)
        act_t = act_t.rearrange("p (t r) -> p t r", t=KT2)
        staged = [s.rearrange("p (k n c) -> p k n c", k=KT1, n=GP) for s in (staged0, staged1)]
        y_sb = [y_sb0, y_sb1]

        def w1_slot(k):
            return ring[:, k * SLOT:k * SLOT + W1C].rearrange("p (k f) -> p k f", k=KT1)

        def w2_slot(k):
            return ring[:, k * SLOT + W1C:(k + 1) * SLOT].rearrange("p (e t d) -> p e t d", e=2, t=KT2)

        EARLY_SLOT = 6
        (probs, q_diag, xa_t, q_t, k_t, xn_t, yn_t), end = carve(
            ring, EARLY_SLOT * SLOT + W1C, [2 * H * S, H * S, 2 * J * S, 2 * J * S, 2 * J * S, 2 * J * S, 2 * S])
        assert end <= SLOTS * SLOT, end
        (ids, phi_sq, phi_w, b1_sb), _ = carve(probs, 0, [6 * S, 2 * NE, 4 * NE, F])
        (emb, emb_sum, xa, v_aug, xn, yn, pv_sb, exp_d, log_t, disp, disp_t, log_c, exp_c, comb, w_qkv, w_o, mask,
         head_mask, phi_sb, phi_n, gam, bet, small, ones), end = carve(
            late, 0, [3 * J * D, J * D, J * D, J * H * 32, J * D, D, 3 * S, P, P, P, P, J * NE, J * NE, 2 * J * NE,
                      2 * 3 * D, 2 * D, S, HH, 2 * NE, 2 * NE, D, D, 166, HD])
        assert end <= LATE, end
        emb = emb.rearrange("p (t j d) -> p t j d", t=3, j=J)
        emb_sum = emb_sum.rearrange("p (j d) -> p j d", j=J)
        xa = xa.rearrange("p (j d) -> p j d", j=J)
        xa_t = xa_t.rearrange("p (c m) -> p c m", c=2)
        q_t = q_t.rearrange("p (c m) -> p c m", c=2)
        k_t = k_t.rearrange("p (c m) -> p c m", c=2)
        q_diag = q_diag.rearrange("p (g h m) -> p g h m", g=2, h=HH)
        v_aug = v_aug.rearrange("p (j h e) -> p j h e", j=J, h=H)
        probs = probs.rearrange("p (u h m) -> p u h m", u=2, h=H)
        xn = xn.rearrange("p (j d) -> p j d", j=J)
        xn_t = xn_t.rearrange("p (c m) -> p c m", c=2)
        yn_t = yn_t.rearrange("p (c m) -> p c m", c=2)
        disp_t, log_c, exp_c = (a.rearrange("p (j n) -> p j n", j=J) for a in (disp_t, log_c, exp_c))
        comb = comb.rearrange("p (j r n) -> p j r n", j=J, r=2)
        w_qkv = w_qkv.rearrange("p (c n) -> p c n", c=2)
        w_o = w_o[0:HD, :].rearrange("p (c n) -> p c n", c=2)
        ids_f = ids[:, 2 * S:5 * S].rearrange("p (t m) -> p t m", t=3)
        ids_w = ids[:, 5 * S:6 * S]
        phi_n2 = phi_n.rearrange("p (c n) -> p c n", c=2)
        phi_sb, phi_sq = (a.rearrange("p (c n) -> p c n", c=2) for a in (phi_sb, phi_sq))

        psum = ctx.enter_context(nc.psum_tensor("psum", [P, 8, 512], F32))
        PV_BANK, Y_BANK, WO_BANK, SHARED_BANK = 3, 4, 5, 6

        ids_loaded = sem("ids_loaded")
        norm_loaded = sem("norm_loaded")
        wqkv_loaded = sem("wqkv_loaded")
        wo_loaded = sem("wo_loaded")
        phi_loaded = sem("phi_loaded")
        b1_loaded = sem("b1_loaded")
        b2_loaded = sem("b2_loaded")
        consts_ready = sem("consts_ready")
        ids_fixed = sem("ids_fixed")
        ids_turned = sem("ids_turned")
        ids_ready = sem("ids_ready")
        ids_staged = sem("ids_staged")
        gathered = sem("gathered")
        emb_summed = sem("emb_summed")
        emb_normed = sem("emb_normed")
        scaled = sem("scaled")
        hidden_ready = sem("hidden_ready")
        xa_ready = sem("xa_ready")
        phi_squared = sem("phi_squared")
        phi_summed = sem("phi_summed")
        phi_ready = sem("phi_ready")
        qk_copied = sem("qk_copied")
        b1_turned = sem("b1_turned")
        b1_ready = sem("b1_ready")
        shared_full = [sem(f"shared_full{i}") for i in range(2)]
        shared_free = [sem(f"shared_free{i}") for i in range(2)]
        diag_ready = sem("diag_ready")
        scores_done = sem("scores_done")
        squared = sem("squared")
        masked = sem("masked")
        pv_done = sem("pv_done")
        pv_copied = sem("pv_copied")
        y_turned = sem("y_turned")
        y_normed = sem("y_normed")
        yn_turned = sem("yn_turned")
        yn_copied = sem("yn_copied")
        wo_done = sem("wo_done")
        attended = sem("attended")
        xn_ready = sem("xn_ready")
        max_d_ready = sem("max_d_ready")
        exp_d_ready = sem("exp_d_ready")
        disp_ready = sem("disp_ready")
        log_c_ready = sem("log_c_ready")
        exp_c_ready = sem("exp_c_ready")
        comb_ready = sem("comb_ready")
        waits_apart = sem("waits_apart")
        zeroed = sem("zeroed")
        vec_step = sem("vec_step")
        w1_loaded = [sem(f"w1_loaded{k}") for k in range(SLOTS)]
        w2_loaded = [sem(f"w2_loaded{k}") for k in range(SLOTS)]
        slots_staged = sem("slots_staged")
        w1_used = sem("w1_used")
        w2_used = sem("w2_used")
        h_copied = sem("h_copied")
        h_turned = sem("h_turned")
        bias_added = sem("bias_added")
        act_ready = sem("act_ready")
        y_low = sem("y_low")
        y_ready = sem("y_ready")
        y_stored = [sem(f"y_stored{i}") for i in range(2)]
        y_loaded = sem("y_loaded")
        combined = sem("combined")
        added = sem("added")
        out_stored = sem("out_stored")

        y_dram = nc.dram_tensor("slot_outputs", [NE * B, D], F32, kind="Internal").ap()

        nexts, prevs = len(PROJECT), len([s for s in ORDER if "~" in s])
        both = (nexts + prevs) // 2
        before_loop = 2 * (nexts // 2)

        def shared(stage, c):
            mark_free = [s for s in ORDER if (runs_next(c) or "'" not in s) and (runs_prev(c) or "~" not in s)]
            bank, before = shared_uses(PROJECT if c is None else mark_free)[stage]
            if c is None:
                return bank, before
            if type(c) is int and c == 0:
                return bank, nexts // 2 + before
            if type(c) is int and c == NC:
                return bank, before_loop + both * (NC - 2) + prevs // 2 + before
            return bank, c * both + (before_loop - both + before)

        def runs_self(c):
            return type(c) is not int or c < NC

        def runs_next(c):
            return type(c) is not int or c < NC - 1

        def runs_embed(c):
            return type(c) is not int or c < NC - 2

        def runs_prev(c):
            return type(c) is not int or c > 0

        def couples(eng, body):
            body(0)
            with eng.Fori(1, NC - 2) as c:
                body(c)
            body(NC - 2)
            body(NC - 1)
            body(NC)

        def runs(stage, c):
            if "'" in stage:
                return runs_next(c)
            return runs_prev(c) if "~" in stage else runs_self(c)

        def wait_free(eng, stage, c):
            bank, before = shared(stage, c)
            eng.wait_ge(shared_free[bank], before + 1)

        def first(i):
            return type(i) is int and i == 0

        def groups(eng, group):
            group(0, 0)
            group(0, 1)
            with eng.Fori(1, NG // 2) as i:
                group(i, 0)
                group(i, 1)

        def apart(eng):
            eng.sem_inc(waits_apart, 1)

        def turn(pe, to, of, rows):
            return pe.transpose(to, of, ident[0:rows, 0:rows])

        block = ctx.enter_context(nc.Block())

        @block.sync
        def _(sp):
            raw = ids.bitcast(I32)
            sp.dma_start(raw[0:B, 0:S], x).then_inc(ids_loaded, 16)
            sp.dma_start(raw[0:B, S:2 * S], types).then_inc(ids_loaded, 16)
            sp.dma_start(gam, gamma.rearrange("(o d) -> o d", o=1).to_broadcast([P, D])).then_inc(norm_loaded, 16)
            sp.dma_start(bet, beta.rearrange("(o d) -> o d", o=1).to_broadcast([P, D])).then_inc(norm_loaded, 16)
            sp.dma_start(phi_sb[0:HD], phi.rearrange("(c p) n o -> p c (n o)", c=2)).then_inc(phi_loaded, 16)
            sp.dma_start(phi_w[0:HD, 3 * NE:3 * NE + 1],
                         scale.rearrange("(o d) -> o d", o=1).to_broadcast([HD, 1])).then_inc(phi_loaded, 16)
            sp.dma_start(b1_sb[0:NE, :], b1).then_inc(b1_loaded, 16)
            for n, w in enumerate((wq, wk, wv)):
                sp.dma_start(w_qkv[0:HD, :, n * D:(n + 1) * D],
                             w.rearrange("(c p) n -> p c n", c=2)).then_inc(wqkv_loaded, 16)
            sp.dma_start(w_o, wo.rearrange("(c p) n -> p c n", c=2)).then_inc(wo_loaded, 16)

            w1_pairs = w1.rearrange("(n e) k f -> n (e k) f", e=2).rearrange("n (k p) f -> n p k f", p=P)
            w2_pairs = w2.rearrange("(n e) (p t) d -> n p e t d", e=2, t=KT2)

            def load_w1(slot, pair):
                sp.dma_start(w1_slot(slot), pair).then_inc(w1_loaded[slot], 16)

            def load_w2(slot, pair):
                sp.dma_start(w2_slot(slot), pair).then_inc(w2_loaded[slot], 16)

            for slot in range(EARLY_SLOT + 1):
                sp.wait_ge(gathered, 16 * 3 * J * min(slot + 3, NC))
                load_w1(slot, w1_pairs[slot])
                if slot < EARLY_SLOT:
                    load_w2(slot, w2_pairs[slot])
            wait_free(sp, "CT~", NC)
            load_w1(SLOTS - 1, w1_pairs[SLOTS - 1])
            for slot in range(EARLY_SLOT, SLOTS):
                load_w2(slot, w2_pairs[slot])
            sp.dma_start(slot_out[NE:P], b2.unsqueeze(1).to_broadcast([NE, B, D])).then_inc(b2_loaded, 16)

            with sp.Fori(1, NG // 2) as i:
                for u in range(2):
                    sp.wait_ge(w1_used, 2 * i + (u - 1))
                    for slot in range(GP * u, GP * (u + 1)):
                        load_w1(slot, w1_pairs[bass.ds(i * SLOTS + slot, 1)].squeeze(0))
                    sp.wait_ge(w2_used, 2 * i + (u - 1))
                    for slot in range(GP * u, GP * (u + 1)):
                        load_w2(slot, w2_pairs[bass.ds(i * SLOTS + slot, 1)].squeeze(0))
            for i in range(2):
                sp.wait_ge(y_stored[i], 16 * (NG // 2))
            sp.dma_start(slot_out[0:NE], y_dram.rearrange("(n b) d -> n b d", b=B)).then_inc(y_loaded, 16)
            for c in range(NC):
                sp.wait_ge(added, J * (c + 1))
                sp.dma_start(out[J * c:J * (c + 1)].rearrange("b m d -> m b d"),
                             hidden[:, J * c:J * (c + 1), :]).then_inc(out_stored, 16)
            sp.wait_ge(out_stored, 16 * NC)

        @block.gpsimd
        def _(pool):
            pool.memset(ident, 0.0).then_inc(zeroed, 1)
            pool.memset(mask, 1.0).then_inc(zeroed, 1)
            pool.memset(head_mask[0:HD, :], 1.0).then_inc(zeroed, 1)
            pool.memset(ones[0:HD, :], 1.0).then_inc(consts_ready, 1)
            pool.wait_ge(zeroed, 3)
            pool.affine_select(out=ident, in_=ident, compare_op=ALU.not_equal, fill=1.0, base=0,
                               pattern=[[-1, P]], channel_multiplier=1).then_inc(consts_ready, 1)
            pool.affine_select(out=mask, in_=mask, compare_op=ALU.is_ge, fill=0.0, base=0,
                               pattern=[[1, S]], channel_multiplier=-1).then_inc(consts_ready, 1)
            pool.affine_select(out=head_mask[0:HD, :], in_=head_mask[0:HD, :], compare_op=ALU.is_ge, fill=0.0,
                               base=0, pattern=[[-FD, HH]], channel_multiplier=1).then_inc(zeroed, 1)
            pool.wait_ge(zeroed, 4)
            pool.affine_select(out=head_mask[0:HD, :], in_=head_mask[0:HD, :], compare_op=ALU.is_ge, fill=0.0,
                               base=FD - 1, pattern=[[FD, HH]], channel_multiplier=-1).then_inc(consts_ready, 1)
            pool.iota(odd, pattern=[[0, 1]], base=0, channel_multiplier=1).then_inc(consts_ready, 1)
            pool.memset(v_aug[:, :, :, FD:32], 1.0).then_inc(consts_ready, 1)
            pool.memset(slots_t, 0.0).then_inc(consts_ready, 1)

            pool.wait_ge(norm_loaded, 32)
            pool.wait_ge(ids_ready, 1)
            id_all = small[:, 0:3 * B].bitcast(U32).rearrange("p (t b) -> p t b", t=3)
            id_couple = small[:, 48:48 + 3 * J].bitcast(U32).rearrange("p (t j) -> p t j", t=3)

            def gather(k):
                if not first(k):
                    pool.wait_ge(emb_summed, k)
                pool.tensor_copy(id_couple, id_all[:, :, bass.ds(k * J, J)]).then_inc(ids_staged, 1)
                pool.wait_ge(ids_staged, k + 1)
                apart(pool)
                for t, table in enumerate((tok_table, pos_table, type_table)):
                    for j in range(J):
                        pool.indirect_dma_start(
                            out=emb[:, t, j, :], out_offset=None, in_=table,
                            in_offset=bass.IndirectOffsetOnAxis(ap=id_couple[:, t, j:j + 1], axis=0),
                        ).then_inc(gathered, 16)

            def scale_shift(k):
                part = hidden[:, bass.ds(k * J, J), :]
                pool.wait_ge(emb_normed, k + 1)
                pool.tensor_tensor(part, part, gam.unsqueeze(1).to_broadcast([P, J, D]), ALU.mult)\
                    .then_inc(scaled, 1)
                pool.wait_ge(scaled, k + 1)
                apart(pool)
                pool.tensor_tensor(part, part, bet.unsqueeze(1).to_broadcast([P, J, D]), ALU.add)\
                    .then_inc(hidden_ready, 1)

            gather(0)
            with pool.Fori(0, NC - 1) as k:
                gather(k + 1)
                scale_shift(k)
            scale_shift(NC - 1)

            wait_free(pool, "XS~", NC)
            wait_free(pool, "CT~", NC)

            def stage(i, u):
                if not first(i):
                    pool.wait_ge(w1_used, 2 * i + (u - 1))
                pool.tensor_copy(staged[u], slots_t[:, :, bass.ds(i * SLOTS + GP * u, GP), :])\
                    .then_inc(slots_staged, 1)

            groups(pool, stage)

        @block.tensor
        def _(pe):
            pe.wait_ge(consts_ready, 7)

            def project(stage, c):
                bank, before = shared(stage, c)
                to = psum[:, SHARED_BANK + bank, :]
                if type(before) is not int or before > 0:
                    pe.wait_ge(shared_free[bank], before)
                if stage == "XT'":
                    pe.wait_ge(xa_ready, 1 if c is None else c + 2)
                    for half in range(2):
                        for j in range(J):
                            mm = turn(pe, to[0:HD, (half * J + j) * S:(half * J + j + 1) * S],
                                      xa[:, j, half * HD:(half + 1) * HD], P)
                elif stage[:2] == "QK":
                    wait_free(pe, "XT'", c)
                    for half in range(2):
                        at = int(stage[2]) * D + half * HD
                        for k in range(2):
                            mm = pe.matmul(to[0:HD, half * J * S:(half + 1) * J * S], w_qkv[0:HD, k, at:at + HD],
                                           xa_t[0:HD, k, :], start=(k == 0), stop=(k == 1))
                else:
                    for j in range(J):
                        for k in range(2):
                            mm = pe.matmul(to[:, j * D:(j + 1) * D], xa_t[0:HD, k, j * S:(j + 1) * S],
                                           w_qkv[0:HD, k, 2 * D:3 * D], start=(k == 0), stop=(k == 1))
                mm.then_inc(shared_full[bank], 1)

            def scores(c, j):
                b = c * J + j
                if j == 0:
                    pe.wait_ge(qk_copied, 2 * (c + 1))
                for m, (bank, g, h0, n) in enumerate([(0, 0, 0, 4), (1, 0, 4, 2), (1, 1, 0, 2), (2, 1, 2, 4)]):
                    pe.wait_ge(diag_ready, 2 * b + (g + 1))
                    if not first(b) and m != 2:
                        pe.wait_ge(squared, 3 * b + (bank - 2))
                    at = {0: 0, 1: 0, 2: 2 * S, 3: 0}[m]
                    pe.matmul(psum[:, bank, at:at + n * S], k_t[0:HD, g, j * S:(j + 1) * S],
                              q_diag[0:HD, g, h0:h0 + n, :], start=True, stop=True,
                              skip_group_check=True).then_inc(scores_done, 1)

            def weigh(c, j):
                b = c * J + j
                if not first(b):
                    pe.wait_ge(pv_copied, b)
                for h in range(H):
                    if h % 4 == 0:
                        pe.wait_ge(masked, 3 * b + (h // 4 + 1))
                    at = 32 * (h % 4)
                    mm = pe.matmul(psum[at:at + 32, PV_BANK, (h // 4) * S:(h // 4 + 1) * S], v_aug[:, j, h, :],
                                   probs[:, j, h, :], start=True, stop=True, skip_group_check=True)
                mm.then_inc(pv_done, 1)

            def turn_y(c, j):
                b = c * J + j
                pe.wait_ge(pv_copied, b + 1)
                if not first(b):
                    pe.wait_ge(yn_copied, b)
                for k in range(3):
                    mm = turn(pe, psum[:, Y_BANK, k * S:(k + 1) * S], pv_sb[:, k * S:(k + 1) * S], P)
                mm.then_inc(y_turned, 1)

            def turn_yn(c, j):
                pe.wait_ge(y_normed, c * J + (j + 1))
                for k in range(2):
                    mm = turn(pe, psum[0:HD, Y_BANK, k * S:(k + 1) * S], yn[:, k * HD:(k + 1) * HD], P)
                mm.then_inc(yn_turned, 1)

            def project_out(c, j):
                b = c * J + j
                pe.wait_ge(yn_copied, b + 1)
                if not first(b):
                    pe.wait_ge(attended, b)
                for k in range(2):
                    mm = pe.matmul(psum[:, WO_BANK, 0:D], yn_t[0:HD, k, :], w_o[:, k, :],
                                   start=(k == 0), stop=(k == 1))
                mm.then_inc(wo_done, 1)

            def route(stage, c):
                bank, before = shared(stage, c)
                to = psum[:, SHARED_BANK + bank, :]
                pe.wait_ge(shared_free[bank], before)
                if stage == "XN~":
                    pe.wait_ge(xn_ready, c)
                    for half in range(2):
                        for j in range(J):
                            mm = turn(pe, to[0:HD, (half * J + j) * S:(half * J + j + 1) * S],
                                      xn[:, j, half * HD:(half + 1) * HD], P)
                elif stage == "LT~":
                    wait_free(pe, "XN~", c)
                    for j in range(J):
                        for k in range(2):
                            mm = pe.matmul(to[NE * j:NE * (j + 1), 0:S], phi_n2[0:HD, k, :],
                                           xn_t[0:HD, k, j * S:(j + 1) * S], start=(k == 0), stop=(k == 1),
                                           skip_group_check=True)
                elif stage == "LN~":
                    wait_free(pe, "LT~", c)
                    mm = turn(pe, to[:, 0:P], log_t, P)
                elif stage == "DT~":
                    pe.wait_ge(disp_ready, c)
                    mm = turn(pe, to[:, 0:P], disp, P)
                elif stage == "XS~":
                    wait_free(pe, "DT~", c)
                    for j in range(J):
                        even, oddn = disp_t[:, j, 0:NE:2], disp_t[:, j, 1:NE:2]
                        for rows, tile, lo, hi, rhs in ((slice(0, P), 0, 0, P, even), (slice(0, P), 1, D - P, D, oddn),
                                                        (slice(0, NE), 2, P, D, even), (slice(NE, P), 2, 0, D - P, oddn)):
                            at = (tile * J + j) * NPAIR
                            mm = pe.matmul(to[rows, at:at + NPAIR], xn[:, j, lo:hi], rhs,
                                           start=True, stop=True, skip_group_check=True)
                else:
                    pe.wait_ge(comb_ready, c)
                    for j in range(J):
                        mm = turn(pe, to[:, j * S:(j + 1) * S], comb[:, j].rearrange("p r n -> p (r n)"), P)
                mm.then_inc(shared_full[bank], 1)

            attend = {"S": scores, "PV": weigh, "YT": turn_y, "YN": turn_yn, "WO": project_out}

            def body(c):
                for stage in ORDER:
                    if not runs(stage, c):
                        continue
                    if "'" in stage:
                        project(stage, c)
                    elif "~" in stage:
                        route(stage, c)
                    else:
                        attend[stage[:-1]](c, int(stage[-1]))

            pe.wait_ge(ids_fixed, 1)
            for t in range(3):
                mm = turn(pe, psum[:, Y_BANK, t * B:(t + 1) * B], ids_f[0:B, t, :], B)
            mm.then_inc(ids_turned, 1)
            pe.wait_ge(phi_squared, 1)
            for c in range(2):
                mm = pe.matmul(psum[0:HD, WO_BANK, 0:NE], ones[0:HD, :], phi_sq[0:HD, c, :],
                               start=(c == 0), stop=(c == 1))
            mm.then_inc(phi_summed, 1)
            pe.wait_ge(b1_loaded, 16)
            for t in range(KT2):
                mm = turn(pe, psum[:, PV_BANK, t * NE:(t + 1) * NE], b1_sb[0:NE, t:F:KT2], NE)
            mm.then_inc(b1_turned, 1)

            pe.wait_ge(wqkv_loaded, 48)
            for stage in PROJECT:
                project(stage, None)
            pe.wait_ge(wo_loaded, 16)
            pe.wait_ge(phi_ready, 1)
            pe.wait_ge(b1_ready, 1)
            couples(pe, body)

            def group(i, u):
                g = 2 * i + u
                pe.wait_ge(slots_staged, g + 1)
                for k in range(GP):
                    pe.wait_ge(w1_loaded[GP * u + k], 16 * (i + 1))
                for kt in range(KT1):
                    for half in range(2):
                        for k in range(GP):
                            mm = pe.matmul(psum[32 * k:32 * k + 32, half, 0:F // 2], staged[u][:, kt, k, :],
                                           w1_slot(GP * u + k)[:, kt, half * (F // 2):(half + 1) * (F // 2)],
                                           start=(kt == 0), stop=(kt == KT1 - 1), skip_group_check=True)
                mm.then_inc(w1_used, 1)
                pe.wait_ge(h_copied, 2 * g + 2)
                for t in range(KT2):
                    mm = turn(pe, psum[:, 2 + t // 4, (t % 4) * P:(t % 4 + 1) * P], h_sb[:, t, :], P)
                    if t in (3, KT2 - 1):
                        mm.then_inc(h_turned, 1)
                for k in range(GP):
                    pe.wait_ge(w2_loaded[GP * u + k], 16 * (i + 1))
                if u or not first(i):
                    pe.wait_ge(y_ready, g)
                for t in range(KT2):
                    if t in (0, 4):
                        pe.wait_ge(act_ready, 2 * g + (1 if t == 0 else 2))
                    for k in range(GP):
                        mm = pe.matmul(psum[32 * k:32 * k + 32, 4, 0:2 * D], act_t[:, t, 32 * k:32 * k + 32],
                                       w2_slot(GP * u + k)[:, :, t, :], start=(t == 0), stop=(t == KT2 - 1),
                                       skip_group_check=True)
                mm.then_inc(w2_used, 1)

            groups(pe, group)

            pe.wait_ge(b2_loaded, 16)
            pe.wait_ge(y_loaded, 16)
            for b in range(B):
                if b >= 8:
                    pe.wait_ge(added, b - 7)
                pe.matmul(psum[:, b % 8, 0:D], combine_t[:, b, :], slot_out[:, b, :],
                          start=True, stop=True).then_inc(combined, 1)

        @block.vector
        def _(dve):
            BEFORE, BODY = 94, 32
            base, done = [0], [0]

            def tick(ins):
                done[0] += 1
                ins.then_inc(vec_step, 1)

            def settle():
                dve.wait_ge(vec_step, base[0] + done[0])

            def step(ins):
                tick(ins)
                settle()

            def rsqrt(y, v, t):
                step(dve.tensor_scalar(y.bitcast(I32), v.bitcast(I32), 1, None, ALU.logical_shift_right))
                step(dve.tensor_scalar(y.bitcast(I32), y.bitcast(I32), -1.0, MAGIC, ALU.mult, ALU.add))
                for _ in range(3):
                    step(dve.scalar_tensor_tensor(out=t, in0=v, scalar=-0.5, in1=y, op0=ALU.mult, op1=ALU.mult))
                    step(dve.tensor_tensor(t, t, y, ALU.mult))
                    step(dve.scalar_tensor_tensor(out=y, in0=t, scalar=1.5, in1=y, op0=ALU.add, op1=ALU.mult))

            EMB, ATT, ROU = 0, J, 2 * J
            stats = small[:, 60:96].rearrange("p (j s) -> p j s", s=6)
            mv = small[:, 96:108].rearrange("p (j s) -> p j s", s=2)
            vs, rs, tmp = small[:, 108:116], small[:, 116:124], small[:, 124:132]
            max_d, den_d, rec_d = small[:, 132:133], small[:, 133:134], small[:, 134:135]
            max_c, den_c, rec_c = small[:, 136:138], small[:, 138:140], small[:, 140:142]
            den_y, rec_y = small[:, 142:154], small[:, 154:166]

            def statistics(e, a, r):
                def bn(at, rows):
                    for j in range(J):
                        ins = dve.bn_stats(stats[:, at + j, :], rows(j))
                    return ins

                def row(k):
                    return lambda j: hidden[:, bass.ds(k * J + j, 1), :]

                for k, done_rows in ((e, emb_normed), (a, xa_ready), (r, xn_ready)):
                    if k is not None and not first(k):
                        dve.wait_ge(done_rows, k)
                if e is not None:
                    dve.wait_ge(gathered, 16 * 3 * J * (e + 1))
                    tick(dve.tensor_tensor(emb_sum, emb[:, 0], emb[:, 1], ALU.add))
                if a is not None:
                    dve.wait_ge(hidden_ready, a + 1)
                    apart(dve)
                    ins = bn(ATT, row(a))
                if e is not None:
                    settle()
                    dve.tensor_tensor(emb_sum, emb_sum, emb[:, 2], ALU.add).then_inc(emb_summed, 1)
                if r is not None:
                    dve.wait_ge(attended, J * (r + 1))
                    apart(dve)
                    ins = bn(ROU, row(r))
                if e is not None:
                    dve.wait_ge(emb_summed, e + 1)
                    apart(dve)
                    ins = bn(EMB, lambda j: emb_sum[:, j, :])
                step(ins)
                apart(dve)
                for at, k in ((ATT, a), (ROU, r), (EMB, e)):
                    if k is not None:
                        for j in range(J):
                            ins = dve.bn_aggr(mv[:, at + j, :], stats[:, at + j, :])
                step(ins)
                if e is not None:
                    tick(dve.tensor_scalar(vs[:, EMB:EMB + J], mv[:, EMB:EMB + J, 1], 1e-12, None, ALU.add))
                if a is not None:
                    tick(dve.tensor_scalar(vs[:, ATT:ATT + J], mv[:, ATT:ATT + J, 1], 1e-5, None, ALU.add))
                if r is not None:
                    tick(dve.tensor_scalar(vs[:, ROU:ROU + J], mv[:, ROU:ROU + J, 1], 1e-5, None, ALU.add))
                    tick(dve.tensor_scalar(vs[:, ROU + J:], mv[:, ROU:ROU + J, 1], float(D), None, ALU.mult))
                settle()

            def normalise(e, a, r, between=lambda: None):
                def rows(k, out, source, at, scale_by, ready):
                    if k is None:
                        return
                    for j in range(J):
                        ins = dve.tensor_scalar(out(j), source(j), mv[:, at + j, 0:1], scale_by(j),
                                                ALU.subtract, ALU.mult)
                    ins.then_inc(ready, 1)

                rsqrt(rs, vs, tmp)
                length, rstd_r, inverse = tmp[:, 0:J], rs[:, ROU:ROU + J], tmp[:, J:2 * J]
                if r is not None:
                    tick(dve.tensor_tensor(length, vs[:, ROU + J:], rs[:, ROU + J:], ALU.mult))
                    settle()
                    step(dve.tensor_tensor(length, length, rstd_r, ALU.mult))
                    step(dve.tensor_scalar(length, length, 1e-12, None, ALU.max))
                    tick(dve.reciprocal(inverse, length))
                    settle()
                    step(dve.tensor_tensor(rstd_r, rstd_r, inverse, ALU.mult))
                rows(r, lambda j: xn[:, j:j + 1, :], lambda j: hidden[:, bass.ds(r * J + j, 1), :], ROU,
                     lambda j: rs[:, ROU + j:ROU + j + 1], xn_ready)
                between()
                rows(a, lambda j: xa[:, j:j + 1, :], lambda j: hidden[:, bass.ds(a * J + j, 1), :], ATT,
                     lambda j: rs[:, ATT + j:ATT + j + 1], xa_ready)
                rows(e, lambda j: hidden[:, bass.ds(e * J + j, 1), :], lambda j: emb_sum[:, j:j + 1, :], EMB,
                     lambda j: rs[:, EMB + j:EMB + j + 1], emb_normed)

            def diagonal(c, j):
                b = c * J + j
                if j == 0:
                    dve.wait_ge(qk_copied, 2 * c + 1)
                for g in range(2):
                    if not first(b):
                        dve.wait_ge(scores_done, 4 * b - 2 + 2 * g)
                    dve.tensor_tensor(
                        q_diag[0:HD, g], q_t[0:HD, g, j * S:(j + 1) * S].unsqueeze(1).to_broadcast([HD, HH, S]),
                        head_mask[0:HD, :].unsqueeze(2).to_broadcast([HD, HH, S]), ALU.mult).then_inc(diag_ready, 1)

            def mask_scores(c, j):
                b = c * J + j
                for k in range(3):
                    part = probs[:, j, 4 * k:4 * k + 4, :]
                    dve.wait_ge(squared, 3 * b + (k + 1))
                    dve.scalar_tensor_tensor(out=part, in0=part, scalar=1.0,
                                             in1=mask.unsqueeze(1).to_broadcast([P, 4, S]),
                                             op0=ALU.add, op1=ALU.mult).then_inc(masked, 1)

            def normalise_y(c, j):
                dve.wait_ge(y_turned, c * J + (j + 1))
                heads = psum[:, Y_BANK, 0:3 * S].rearrange("p (h e) -> p h e", e=32)
                step(dve.tensor_scalar(den_y, heads[:, :, FD], 2e-12, None, ALU.add))
                step(dve.reciprocal(rec_y, den_y))
                dve.tensor_tensor(yn.rearrange("p (h e) -> p h e", e=FD), heads[:, :, 0:FD],
                                  rec_y.unsqueeze(2).to_broadcast([P, H, FD]), ALU.mult).then_inc(y_normed, 1)

            def add_attention(c, j):
                b = c * J + j
                dve.wait_ge(wo_done, b + 1)
                row = hidden[:, bass.ds(b, 1), :]
                dve.tensor_tensor(row, row, psum[:, WO_BANK, 0:D].unsqueeze(1), ALU.add).then_inc(attended, 1)

            def dispatch_max(c):
                bank, before = shared("LT~", c)
                dve.wait_ge(shared_full[bank], before + 1)
                dve.tensor_reduce(max_d, psum[:, SHARED_BANK + bank, 0:S], AX.X, ALU.max, negate=True)\
                    .then_inc(max_d_ready, 1)

            def dispatch_norm(c):
                dve.wait_ge(exp_d_ready, c)
                step(dve.reciprocal(rec_d, den_d))
                dve.tensor_scalar(disp, exp_d, rec_d, None, ALU.mult).then_inc(disp_ready, 1)

            def combine_max(c):
                bank, before = shared("LN~", c)
                dve.wait_ge(shared_full[bank], before + 1)
                logits = psum[:, SHARED_BANK + bank, 0:P].rearrange("p (j n) -> p j n", j=J)
                step(dve.tensor_reduce(max_c, logits, AX.X, ALU.max))
                step(dve.tensor_tensor(log_c, logits, max_c.unsqueeze(2).to_broadcast([P, J, NE]), ALU.subtract))
                dve.sem_inc(shared_free[bank], 1)
                dve.sem_inc(log_c_ready, 1)

            def combine_norm(c):
                dve.wait_ge(exp_c_ready, c)
                step(dve.tensor_reduce(den_c, exp_c, AX.X, ALU.add))
                step(dve.reciprocal(rec_c, den_c))
                dve.tensor_tensor(comb, exp_c.unsqueeze(2).to_broadcast([P, J, 2, NE]),
                                  rec_c.unsqueeze(2).unsqueeze(3).to_broadcast([P, J, 2, NE]), ALU.mult)\
                    .then_inc(comb_ready, 1)

            def body(c):
                if type(c) is not int:
                    assert done[0] == BEFORE, done[0]
                    base[0], done[0] = c * BODY + (BEFORE - BODY), 0
                here, prev = runs_self(c), runs_prev(c)
                those = (c + 2 if runs_embed(c) else None, c + 1 if runs_next(c) else None, c - 1 if prev else None)
                if not runs_embed(c):
                    dve.wait_ge(emb_normed, NC)
                if not runs_next(c):
                    dve.wait_ge(xa_ready, NC)
                statistics(*those)
                if here:
                    diagonal(c, 1)
                normalise(*those, between=lambda: mask_scores(c, 0) if here else None)
                if here:
                    mask_scores(c, 1)
                if prev:
                    dispatch_max(c)
                if here:
                    normalise_y(c, 0)
                if prev:
                    dispatch_norm(c)
                    combine_max(c)
                if here:
                    add_attention(c, 0)
                    normalise_y(c, 1)
                if runs_next(c):
                    diagonal(c + 1, 0)
                if prev:
                    combine_norm(c)
                if here:
                    add_attention(c, 1)
                if type(c) is not int:
                    assert done[0] == BODY, done[0]
                    base[0], done[0] = BEFORE + (NC - 3) * BODY, 0

            dve.memset(vs, 1.0).then_inc(vec_step, 1)
            done[0] += 1
            dve.wait_ge(ids_loaded, 32)
            raw = ids.bitcast(I32)
            step(dve.tensor_copy(ids_f[0:B, 0, :], raw[0:B, 0:S]))
            step(dve.tensor_copy(ids_f[0:B, 2, :], raw[0:B, S:2 * S]))
            step(dve.tensor_copy(ids_f[0:B, 1, :], ids_f[0:B, 0, :]))
            for t, n in enumerate(TABLES):
                f = ids_f[0:B, t, :]
                step(dve.tensor_scalar(ids_w[0:B, :], f, 0.0, float(n), ALU.is_lt, ALU.mult))
                step(dve.tensor_tensor(f, f, ids_w[0:B, :], ALU.add))
                step(dve.tensor_scalar(f, f, 0.0, float(n - 1), ALU.max, ALU.min))
            dve.sem_inc(ids_fixed, 1)
            dve.wait_ge(ids_turned, 1)
            dve.tensor_copy(small[:, 0:3 * B].bitcast(U32), psum[:, Y_BANK, 0:3 * B]).then_inc(ids_ready, 1)
            dve.wait_ge(consts_ready, 7)
            step(dve.tensor_scalar(odd, odd, 4, 1, ALU.logical_shift_right, ALU.bitwise_and))

            dve.wait_ge(phi_loaded, 32)
            dve.tensor_tensor(phi_sq[0:HD], phi_sb[0:HD], phi_sb[0:HD], ALU.mult).then_inc(phi_squared, 1)
            dve.wait_ge(phi_summed, 1)
            n2, r, t = (phi_w[0:HD, i * NE:(i + 1) * NE] for i in range(3))
            step(dve.tensor_copy(n2, psum[0:HD, WO_BANK, 0:NE]))
            rsqrt(r, n2, t)
            step(dve.tensor_tensor(t, n2, r, ALU.mult))
            step(dve.tensor_scalar(t, t, 1e-12, None, ALU.max))
            step(dve.reciprocal(r, t))
            step(dve.tensor_scalar(r, r, phi_w[0:HD, 3 * NE:3 * NE + 1], None, ALU.mult))
            dve.tensor_tensor(phi_n2[0:HD], phi_sb[0:HD], r.unsqueeze(1).to_broadcast([HD, 2, NE]), ALU.mult)\
                .then_inc(phi_ready, 1)
            dve.wait_ge(b1_turned, 1)
            dve.tensor_copy(b1_t, psum[:, PV_BANK, 0:KT2 * NE].rearrange("p (t n) -> p t n", t=KT2))\
                .then_inc(b1_ready, 1)

            for k in range(2):
                statistics(k, None, None)
                normalise(k, None, None)
                if k == 0:
                    statistics(None, 0, None)
                    normalise(None, 0, None)
                    dve.wait_ge(xa_ready, 1)
            diagonal(0, 0)
            couples(dve, body)

            def group(i, u):
                g = 2 * i + u
                dve.wait_ge(w1_used, g + 1)
                dve.tensor_copy(h_sb[:, :, P // 2:P].rearrange("p t c -> p c t"),
                                psum[:, 1, 0:F // 2].rearrange("p (c t) -> p c t", t=KT2)).then_inc(h_copied, 1)
                for part, (t0, t1) in enumerate(((0, 4), (4, KT2))):
                    dve.wait_ge(h_turned, 2 * g + (part + 1))
                    dve.tensor_tensor(
                        h_t[:, t0:t1], psum[:, 2 + part, 0:(t1 - t0) * P].rearrange("p (t e b) -> p t e b", e=G, b=B),
                        b1_t[:, t0:t1, bass.ds(g * G, G)].unsqueeze(3).to_broadcast([P, t1 - t0, G, B]),
                        ALU.add).then_inc(bias_added, 1)
                dve.wait_ge(y_low, g + 1)
                apart(dve)
                dve.copy_predicated(y_sb[u], odd.to_broadcast([P, D]), psum[:, 4, D:2 * D]).then_inc(y_ready, 1)

            dve.wait_ge(slots_staged, 1)
            groups(dve, group)

            for b in range(B):
                dve.wait_ge(combined, b + 1)
                dve.tensor_tensor(hidden[:, b, :], hidden[:, b, :], psum[:, b % 8, 0:D], ALU.add)\
                    .then_inc(added, 1)

        @block.scalar
        def _(act):
            def evacuate(stage, c):
                if c is not None and not runs(stage, c):
                    return
                bank, before = shared(stage, c)
                full = psum[:, SHARED_BANK + bank, :]
                act.wait_ge(shared_full[bank], before + 1)
                if stage == "XT'":
                    ins = act.copy(xa_t[0:HD], full[0:HD, :].rearrange("p (h m) -> p h m", h=2))
                elif stage[:2] == "QK":
                    n = int(stage[2])
                    act.copy((q_t, k_t)[n][0:HD], full[0:HD, :].rearrange("p (h m) -> p h m", h=2))\
                        .then_inc(qk_copied, 1)
                    act.wait_ge(qk_copied, n + 1 if c is None else 2 * (c + 1) + (n + 1))
                    act.sem_inc(shared_free[bank], 1)
                    return
                elif stage == "V'":
                    ins = act.copy(v_aug[:, :, :, 0:FD], full[:, 0:J * D].rearrange("p (j h e) -> p j h e", j=J, e=FD))
                elif stage == "XN~":
                    ins = act.copy(xn_t[0:HD], full[0:HD, :].rearrange("p (h m) -> p h m", h=2))
                elif stage == "DT~":
                    ins = act.copy(disp_t, full[:, 0:P].rearrange("p (j n) -> p j n", j=J))
                elif stage == "XS~":
                    part = full[:, 0:3 * J * NPAIR].rearrange("p (t j n) -> p t n j", t=3, j=J)
                    even, oddn = bass.ds(c * J - J, J), bass.ds(c * J + (B - J), J)
                    act.copy(slots_t[:, 0, :, even], part[:, 0])
                    act.copy(slots_t[:, 2, :, oddn], part[:, 1])
                    act.copy(slots_t[0:NE, 1, :, even], part[0:NE, 2])
                    ins = act.copy(slots_t[NE:P, 1, :, oddn], part[NE:P, 2])
                else:
                    ins = act.copy(combine_t[:, bass.ds(c * J - J, J), :],
                                   full[:, 0:J * S].rearrange("p (j m) -> p j m", j=J))
                ins.then_inc(shared_free[bank], 1)

            def square(c, j):
                b = c * J + j
                for k, ready in enumerate((1, 3, 4)):
                    act.wait_ge(scores_done, 4 * b + ready)
                    act.activation(probs[:, j, 4 * k:4 * k + 4, :],
                                   psum[:, k, :].rearrange("p (h m) -> p h m", h=4), ACT.Square,
                                   bias=1.0, scale=0.25).then_inc(squared, 1)

            def copy_pv(c, j):
                act.wait_ge(pv_done, c * J + (j + 1))
                act.copy(pv_sb, psum[:, PV_BANK, 0:3 * S]).then_inc(pv_copied, 1)

            def copy_yn(c, j):
                act.wait_ge(yn_turned, c * J + (j + 1))
                act.copy(yn_t[0:HD], psum[0:HD, Y_BANK, 0:2 * S].rearrange("p (c m) -> p c m", c=2))\
                    .then_inc(yn_copied, 1)

            def dispatch_exp(c):
                if not runs_prev(c):
                    return
                bank, before = shared("LT~", c)
                logits = psum[:, SHARED_BANK + bank, 0:S]
                act.wait_ge(max_d_ready, c)
                act.activation(exp_d, logits, ACT.Exp, bias=max_d, accum_out=den_d).then_inc(exp_d_ready, 1)
                act.copy(log_t, logits).then_inc(shared_free[bank], 1)

            def combine_exp(c):
                if runs_prev(c):
                    act.wait_ge(log_c_ready, c)
                    act.activation(exp_c, log_c, ACT.Exp).then_inc(exp_c_ready, 1)

            def body(c):
                here = runs_self(c)
                if here:
                    square(c, 0)
                    square(c, 1)
                    copy_pv(c, 0)
                evacuate("XN~", c)
                dispatch_exp(c)
                if here:
                    copy_pv(c, 1)
                    copy_yn(c, 0)
                evacuate("XT'", c)
                combine_exp(c)
                evacuate("QK0'", c)
                evacuate("DT~", c)
                if here:
                    copy_yn(c, 1)
                evacuate("XS~", c)
                evacuate("QK1'", c)
                evacuate("CT~", c)
                evacuate("V'", c)

            max_d, den_d = small[:, 132:133], small[:, 133:134]
            act.wait_ge(consts_ready, 7)
            for stage in PROJECT:
                evacuate(stage, None)
            couples(act, body)

            def group(i, u):
                g = 2 * i + u
                act.wait_ge(w1_used, g + 1)
                act.copy(h_sb[:, :, 0:P // 2].rearrange("p t c -> p c t"),
                         psum[:, 0, 0:F // 2].rearrange("p (c t) -> p c t", t=KT2)).then_inc(h_copied, 1)
                for part, (t0, t1) in enumerate(((0, 4), (4, KT2))):
                    act.wait_ge(bias_added, 2 * g + (part + 1))
                    act.activation(act_t[:, t0:t1, :], h_t[:, t0:t1].rearrange("p t e b -> p t (e b)"), ACT.Gelu)\
                        .then_inc(act_ready, 1)
                act.wait_ge(w2_used, g + 1)
                if not first(i):
                    act.wait_ge(y_stored[u], 16 * i)
                act.copy(y_sb[u], psum[:, 4, 0:D]).then_inc(y_low, 1)
                act.wait_ge(y_ready, g + 1)
                act.dma_start(y_dram[bass.ds(g * P, P), :], y_sb[u]).then_inc(y_stored[u], 16)

            groups(act, group)


_INS = ['x', 'mask_BS_i1_0', 'L0_tok_tok_table', 'L0_tok_pos_table', 'L0_tok_type_table', 'L0_tok_gamma',
        'L0_tok_beta', 'L0_attn_Wq', 'L0_attn_Wk', 'L0_attn_Wv', 'L0_attn_Wo', 'L0_ffn_phi', 'L0_ffn_scale',
        'L0_ffn_w1', 'L0_ffn_b1', 'L0_ffn_w2', 'L0_ffn_b2']
_OUT = ((16, 128, 192), 'float32')


def kernel(**inputs):
    import numpy as _np
    import concourse.bacc as _bacc
    from concourse import mybir as _mybir
    from concourse.bass_utils import run_bass_kernel_spmd as _run

    nc = _bacc.Bacc("TRN2", target_bir_lowering=False, num_devices=1)
    arrays, args = {}, []
    for name in _INS:
        a = _np.ascontiguousarray(inputs[name])
        arrays[f"in_{name}_dram"] = a
        args.append(nc.dram_tensor(f"in_{name}_dram", a.shape, _mybir.dt.from_np(a.dtype), kind="ExternalInput").ap())
    shape, dtype = _OUT
    args.append(nc.dram_tensor("out_0_dram", shape, _mybir.dt.from_np(_np.dtype(dtype)), kind="ExternalOutput").ap())
    tower_kernel(nc, *args)
    r = _run(nc, [arrays], core_ids=[0])
    return r.results[0]["out_0_dram"]
```

```python
from contextlib import ExitStack

import concourse.bass as bass
from concourse import mybir

F32 = mybir.dt.float32
I32 = mybir.dt.int32
U32 = mybir.dt.uint32
ACT = mybir.ActivationFunctionType
ALU = mybir.AluOpType
AX = mybir.AxisListType

P = 128
B, S = 16, 128
D = 192
HD = D // 2
H, FD = 12, 16
HH = H // 2
NE, F = 64, 768
NC, J = 8, 2
NPAIR = NE // 2
G = 8
NG = NE // G
EARLY_NE = NE - 2 * G
GP = G // 2
KT1 = 2 * D // P
KT2 = F // P
SLOTS = 2 * GP
W1C = KT1 * F
W2C = 2 * KT2 * D
SLOT = W1C + W2C
LATE = 7620
TABLES = (8000, 128, 2)
MAGIC = float(0x5F3759DF)

PROJECT = ["XT'", "QK0'", "QK1'"]
ORDER = ["S0", "V", "S1", "PV0", "YT0", "XN~", "LT~", "PV1", "YN0", "XT'", "LN~", "WO0", "YT1", "QK0'", "DT~",
         "QK1'", "YN1", "XS~", "WO1", "CT~"]


def shared_uses(order):
    turns = [s for s in order if s[-1] in "'~V"]
    return {s: (n % 2, n // 2) for n, s in enumerate(turns)}, ((len(turns) + 1) // 2, len(turns) // 2)


def tower_kernel(nc, x, types, tok_table, pos_table, type_table, gamma, beta, wq, wk, wv, wo, phi, scale,
                 w1, b1, w2, b2, out):
    with ExitStack() as ctx:
        def sb(name, cols, parts=P):
            return ctx.enter_context(nc.sbuf_tensor(name, [parts, cols], F32))

        def sem(name):
            return ctx.enter_context(nc.semaphore(name))

        ring = sb("ring", SLOTS * SLOT)
        hidden = sb("hidden", B * D)[:, :].rearrange("p (b d) -> p b d", b=B)
        slots_t = sb("slots_t", KT1 * NPAIR * 32)[:, :].rearrange("p (k n c) -> p k n c", k=KT1, n=NPAIR)
        combine_t = sb("combine_t", B * S)[:, :].rearrange("p (b m) -> p b m", b=B)
        ident = sb("ident", P)[:, :]
        b1_t = sb("b1_t", KT2 * NE)[:, :].rearrange("p (t n) -> p t n", t=KT2)
        odd = sb("odd", 1)[:, :].bitcast(I32)
        late = sb("late", LATE)

        def carve(tensor, at, sizes):
            views = []
            for n in sizes:
                views.append(tensor[:, at:at + n])
                at += n
            return views, at

        (slot_out, h_sb, h_t, act_t, staged0, staged1, y_sb0, y_sb1), end = carve(
            late, 0, [B * D, F, F, F, KT1 * GP * 32, KT1 * GP * 32, D, D])
        assert end <= LATE
        slot_out = slot_out.rearrange("p (b d) -> p b d", b=B)
        h_sb = h_sb.rearrange("p (t c) -> p t c", t=KT2)
        h_t = h_t.rearrange("p (t e b) -> p t e b", t=KT2, e=G)
        act_t = act_t.rearrange("p (t r) -> p t r", t=KT2)
        staged = [s.rearrange("p (k n c) -> p k n c", k=KT1, n=GP) for s in (staged0, staged1)]
        y_sb = [y_sb0, y_sb1]
        (last_weights, batch_of_row, b2_rows), end = carve(late, end, [2 * S, B, D])
        assert end <= LATE
        b2_rows = b2_rows[NE:P, :]
        ahead = late[:, 0:W1C].rearrange("p (k f) -> p k f", k=KT1)
        last_weights = last_weights.rearrange("p (u m) -> p u m", u=2)

        def w1_slot(k):
            return ring[:, k * SLOT:k * SLOT + W1C].rearrange("p (k f) -> p k f", k=KT1)

        def w2_slot(k):
            return ring[:, k * SLOT + W1C:(k + 1) * SLOT].rearrange("p (e t d) -> p e t d", e=2, t=KT2)

        spread_weights = [w1_slot(u).rearrange("p k f -> p (k f)")[:, 0:B * S].rearrange("p (b m) -> p b m", b=B)
                          for u in range(2)]
        assert B * S <= W1C

        EARLY_SLOT = 6
        (probs, q_diag, xa_t, q_t, k_t, xn_t, yn_t), end = carve(
            ring, EARLY_SLOT * SLOT + W1C, [2 * H * S, H * S, 2 * J * S, 2 * J * S, 2 * J * S, 2 * J * S, 2 * S])
        assert end <= SLOTS * SLOT, end
        (ids, phi_sq, phi_w, b1_sb, emb_second), end = carve(probs, 0, [6 * S, 2 * NE, 4 * NE, F, 3 * J * D])
        assert end <= 2 * H * S
        (emb, emb_sum, xa, v_aug, xn, yn, pv_sb, exp_d, log_t, disp, disp_t, log_c, exp_c, comb, w_qkv, w_o, mask,
         head_mask, phi_sb, phi_n, gam, bet, small, ones), end = carve(
            late, 0, [3 * J * D, J * D, J * D, J * H * 32, J * D, D, 3 * S, P, P, P, P, J * NE, J * NE, 2 * J * NE,
                      2 * 3 * D, 2 * D, S, HH, 2 * NE, 2 * NE, D, D, 166, HD])
        assert end <= LATE, end
        emb, emb_second = (a.rearrange("p (t j d) -> p t j d", t=3, j=J) for a in (emb, emb_second))
        emb_sum = emb_sum.rearrange("p (j d) -> p j d", j=J)
        xa = xa.rearrange("p (j d) -> p j d", j=J)
        xa_t = xa_t.rearrange("p (c m) -> p c m", c=2)
        q_t = q_t.rearrange("p (c m) -> p c m", c=2)
        k_t = k_t.rearrange("p (c m) -> p c m", c=2)
        q_diag = q_diag.rearrange("p (g h m) -> p g h m", g=2, h=HH)
        v_aug = v_aug.rearrange("p (j h e) -> p j h e", j=J, h=H)
        probs = probs.rearrange("p (u h m) -> p u h m", u=2, h=H)
        xn = xn.rearrange("p (j d) -> p j d", j=J)
        xn_t = xn_t.rearrange("p (c m) -> p c m", c=2)
        yn_t = yn_t.rearrange("p (c m) -> p c m", c=2)
        disp_t, log_c, exp_c = (a.rearrange("p (j n) -> p j n", j=J) for a in (disp_t, log_c, exp_c))
        comb = comb.rearrange("p (j r n) -> p j r n", j=J, r=2)
        w_qkv = w_qkv.rearrange("p (c n) -> p c n", c=2)
        w_o = w_o[0:HD, :].rearrange("p (c n) -> p c n", c=2)
        ids_f = ids[:, 2 * S:5 * S].rearrange("p (t m) -> p t m", t=3)
        ids_w = ids[:, 5 * S:6 * S]
        phi_n2 = phi_n.rearrange("p (c n) -> p c n", c=2)
        phi_sb, phi_sq = (a.rearrange("p (c n) -> p c n", c=2) for a in (phi_sb, phi_sq))

        psum = ctx.enter_context(nc.psum_tensor("psum", [P, 8, 512], F32))
        PV_BANK, Y_BANK, WO_BANK, SHARED_BANK = 3, 4, 5, 6

        ids_loaded = sem("ids_loaded")
        norm_loaded = sem("norm_loaded")
        wqkv_loaded = sem("wqkv_loaded")
        wo_loaded = sem("wo_loaded")
        phi_loaded = sem("phi_loaded")
        b1_loaded = sem("b1_loaded")
        b2_loaded = sem("b2_loaded")
        b2_spread = sem("b2_spread")
        ahead_loaded = sem("ahead_loaded")
        consts_ready = sem("consts_ready")
        ids_fixed = sem("ids_fixed")
        ids_turned = sem("ids_turned")
        ids_ready = sem("ids_ready")
        ids_staged = sem("ids_staged")
        gathered = sem("gathered")
        gathered_second = sem("gathered_second")
        emb_summed = sem("emb_summed")
        emb_normed = sem("emb_normed")
        scaled = sem("scaled")
        hidden_ready = sem("hidden_ready")
        xa_ready = sem("xa_ready")
        phi_squared = sem("phi_squared")
        phi_summed = sem("phi_summed")
        phi_ready = sem("phi_ready")
        qk_copied = sem("qk_copied")
        b1_turned = sem("b1_turned")
        b1_ready = sem("b1_ready")
        shared_full = [sem(f"shared_full{i}") for i in range(2)]
        shared_free = [sem(f"shared_free{i}") for i in range(2)]
        diag_low = sem("diag_low")
        diag_high = sem("diag_high")
        scores_done = sem("scores_done")
        squared = sem("squared")
        masked = sem("masked")
        pv_done = sem("pv_done")
        pv_copied = sem("pv_copied")
        y_turned = sem("y_turned")
        y_normed = sem("y_normed")
        yn_turned = sem("yn_turned")
        yn_copied = sem("yn_copied")
        wo_done = sem("wo_done")
        attended = sem("attended")
        xn_ready = sem("xn_ready")
        max_d_ready = sem("max_d_ready")
        exp_d_ready = sem("exp_d_ready")
        disp_ready = sem("disp_ready")
        log_c_ready = sem("log_c_ready")
        exp_c_ready = sem("exp_c_ready")
        comb_ready = sem("comb_ready")
        waits_apart = sem("waits_apart")
        zeroed = sem("zeroed")
        vec_step = sem("vec_step")
        w1_loaded = [sem(f"w1_loaded{k}") for k in range(SLOTS)]
        w2_loaded = [[sem(f"w2_loaded{half}_{k}") for k in range(SLOTS)] for half in range(2)]
        slots_staged = sem("slots_staged")
        w1_used = sem("w1_used")
        w2_used = sem("w2_used")
        h_copied = sem("h_copied")
        h_turned = sem("h_turned")
        bias_added = sem("bias_added")
        act_ready = sem("act_ready")
        y_low = sem("y_low")
        y_ready = sem("y_ready")
        y_stored = [sem(f"y_stored{i}") for i in range(2)]
        y_loaded = sem("y_loaded")
        rows_zeroed = sem("rows_zeroed")
        weights_stored = sem("weights_stored")
        weights_loaded = sem("weights_loaded")
        weights_spread = sem("weights_spread")
        early_combined = sem("early_combined")
        early_added = sem("early_added")
        combined = sem("combined")
        added = sem("added")
        out_stored = sem("out_stored")

        y_dram = nc.dram_tensor("slot_outputs", [EARLY_NE * B, D], F32, kind="Internal").ap()
        weights_dram = nc.dram_tensor("last_combine_weights", [2 * G, B, S], F32, kind="Internal").ap()

        def order_of(c):
            return PROJECT if c is None else [s for s in ORDER if runs(s, c)]

        def shared(stage, c):
            uses, _ = shared_uses(order_of(c))
            bank, before = uses[stage]
            if c is None or type(c) is int and c in (0, NC):
                bodies = {None: [], 0: [None], NC: [None, 0] + [1] * (NC - 2) + [NC - 1]}[c]
                return bank, before + sum(shared_uses(order_of(k))[1][bank] for k in bodies)
            start = sum(shared_uses(order_of(k))[1][bank] for k in (None, 0))
            each = shared_uses(order_of(1))[1][bank]
            return bank, c * each + (start - each + before)

        def runs_self(c):
            return type(c) is not int or c < NC

        def runs_next(c):
            return type(c) is not int or c < NC - 1

        def runs_embed(c):
            return type(c) is not int or c < NC - 2

        def runs_prev(c):
            return type(c) is not int or c > 0

        def couples(eng, body, peeled=2):
            body(0)
            with eng.Fori(1, NC - peeled) as c:
                body(c)
            for k in range(NC - peeled, NC - 1):
                body(k)
            body(NC - 1)
            body(NC)

        def runs(stage, c):
            if "'" in stage:
                return runs_next(c)
            return runs_prev(c) if "~" in stage else runs_self(c)

        def wait_free(eng, stage, c):
            bank, before = shared(stage, c)
            eng.wait_ge(shared_free[bank], before + 1)

        def diagonal(eng, c, j, g, ready):
            b = c * J + j
            if j == 0:
                eng.wait_ge(qk_copied, 2 * c + 1)
            if not first(b):
                eng.wait_ge(scores_done, 4 * b - 2 + 2 * g)
            eng.tensor_tensor(
                q_diag[0:HD, g], q_t[0:HD, g, j * S:(j + 1) * S].unsqueeze(1).to_broadcast([HD, HH, S]),
                head_mask[0:HD, :].unsqueeze(2).to_broadcast([HD, HH, S]), ALU.mult).then_inc(ready, 1)

        def first(i):
            return type(i) is int and i == 0

        def groups(eng, group):
            group(0, 0)
            group(0, 1)
            with eng.Fori(1, NG // 2 - 1) as i:
                group(i, 0)
                group(i, 1)
            group(NG // 2 - 1, 0)
            group(NG // 2 - 1, 1)

        def is_group(i, u, g):
            return type(i) is int and 2 * i + u == g

        def apart(eng):
            eng.sem_inc(waits_apart, 1)

        def turn(pe, to, of, rows):
            return pe.transpose(to, of, ident[0:rows, 0:rows])

        block = ctx.enter_context(nc.Block())

        @block.sync
        def _(sp):
            raw = ids.bitcast(I32)
            sp.dma_start(raw[0:B, 0:S], x).then_inc(ids_loaded, 16)
            sp.dma_start(raw[0:B, S:2 * S], types).then_inc(ids_loaded, 16)
            sp.dma_start(gam, gamma.rearrange("(o d) -> o d", o=1).to_broadcast([P, D])).then_inc(norm_loaded, 16)
            sp.dma_start(bet, beta.rearrange("(o d) -> o d", o=1).to_broadcast([P, D])).then_inc(norm_loaded, 16)
            sp.dma_start(phi_sb[0:HD], phi.rearrange("(c p) n o -> p c (n o)", c=2)).then_inc(phi_loaded, 16)
            sp.dma_start(phi_w[0:HD, 3 * NE:3 * NE + 1],
                         scale.rearrange("(o d) -> o d", o=1).to_broadcast([HD, 1])).then_inc(phi_loaded, 16)
            sp.dma_start(b1_sb[0:NE, :], b1).then_inc(b1_loaded, 16)
            for n, w in enumerate((wq, wk, wv)):
                sp.dma_start(w_qkv[0:HD, :, n * D:(n + 1) * D],
                             w.rearrange("(c p) n -> p c n", c=2)).then_inc(wqkv_loaded, 16)
            sp.dma_start(w_o, wo.rearrange("(c p) n -> p c n", c=2)).then_inc(wo_loaded, 16)

            w1_pairs = w1.rearrange("(n e) k f -> n (e k) f", e=2).rearrange("n (k p) f -> n p k f", p=P)
            w2_pairs = w2.rearrange("(n e) (p t) d -> n p e t d", e=2, t=KT2)

            def load_w1(slot, pair):
                sp.dma_start(w1_slot(slot), pair).then_inc(w1_loaded[slot], 16)

            def load_w2(slot, pair, halves=(0, 1)):
                for half in halves:
                    t = slice(half * (KT2 // 2), (half + 1) * (KT2 // 2))
                    sp.dma_start(w2_slot(slot)[:, :, t, :], pair[:, :, t, :]).then_inc(w2_loaded[half][slot], 16)

            for slot in range(EARLY_SLOT + 1):
                sp.wait_ge(gathered, 16 * 3 * J * min(slot + 2, NC - 1))
                load_w1(slot, w1_pairs[slot])
                if slot < EARLY_SLOT:
                    load_w2(slot, w2_pairs[slot])
            sp.wait_ge(pv_done, B)
            load_w1(SLOTS - 1, w1_pairs[SLOTS - 1])
            load_w2(EARLY_SLOT, w2_pairs[EARLY_SLOT])
            sp.dma_start(ahead, w1_pairs[SLOTS]).then_inc(ahead_loaded, 16)
            wait_free(sp, "LT~", NC)
            load_w2(SLOTS - 1, w2_pairs[SLOTS - 1])
            wait_free(sp, "CT~", NC)
            sp.dma_start(weights_dram, combine_t[EARLY_NE:NE, :, :]).then_inc(weights_stored, 16)
            sp.wait_ge(weights_stored, 16)
            sp.dma_start(last_weights, weights_dram.rearrange("(u e) b m -> (e b) u m", u=2))\
                .then_inc(weights_loaded, 16)
            sp.dma_start(b2_rows, b2).then_inc(b2_loaded, 16)

            def refill(i):
                for u in range(2):
                    sp.wait_ge(w1_used, 2 * i + (u - 1))
                    for slot in range(GP * u, GP * (u + 1)):
                        if slot >= GP * u + 3:
                            sp.wait_ge(w1_loaded[slot - 3], 16 * (i + 1))
                        if type(i) is int and slot == 0:
                            continue
                        load_w1(slot, w1_pairs[bass.ds(i * SLOTS + slot, 1)].squeeze(0))
                    sp.wait_ge(w2_used, 2 * i + (u - 1))
                    for half in range(2):
                        for slot in range(GP * u, GP * (u + 1)):
                            sp.wait_ge((w2_loaded[0] if half else w1_loaded)[slot], 16 * (i + 1))
                            load_w2(slot, w2_pairs[bass.ds(i * SLOTS + slot, 1)].squeeze(0), (half,))

            refill(1)
            with sp.Fori(2, NG // 2) as i:
                refill(i)
            for c in range(NC):
                sp.wait_ge(added, c + 1)
                sp.dma_start(out[J * c:J * (c + 1)].rearrange("b m d -> m b d"),
                             hidden[:, J * c:J * (c + 1), :]).then_inc(out_stored, 16)
            sp.wait_ge(out_stored, 16 * NC)

        @block.gpsimd
        def _(pool):
            pool.memset(ident, 0.0).then_inc(zeroed, 1)
            pool.memset(mask, 1.0).then_inc(zeroed, 1)
            pool.memset(head_mask[0:HD, :], 1.0).then_inc(zeroed, 1)
            pool.memset(ones[0:HD, :], 1.0).then_inc(consts_ready, 1)
            pool.wait_ge(zeroed, 3)
            pool.affine_select(out=ident, in_=ident, compare_op=ALU.not_equal, fill=1.0, base=0,
                               pattern=[[-1, P]], channel_multiplier=1).then_inc(consts_ready, 1)
            pool.affine_select(out=mask, in_=mask, compare_op=ALU.is_ge, fill=0.0, base=0,
                               pattern=[[1, S]], channel_multiplier=-1).then_inc(consts_ready, 1)
            pool.affine_select(out=head_mask[0:HD, :], in_=head_mask[0:HD, :], compare_op=ALU.is_ge, fill=0.0,
                               base=0, pattern=[[-FD, HH]], channel_multiplier=1).then_inc(zeroed, 1)
            pool.wait_ge(zeroed, 4)
            pool.affine_select(out=head_mask[0:HD, :], in_=head_mask[0:HD, :], compare_op=ALU.is_ge, fill=0.0,
                               base=FD - 1, pattern=[[FD, HH]], channel_multiplier=-1).then_inc(consts_ready, 1)
            pool.iota(odd, pattern=[[0, 1]], base=0, channel_multiplier=1).then_inc(consts_ready, 1)
            pool.memset(v_aug[:, :, :, FD:32], 1.0).then_inc(consts_ready, 1)
            pool.memset(slots_t, 0.0).then_inc(consts_ready, 1)

            pool.wait_ge(norm_loaded, 32)
            pool.wait_ge(ids_ready, 1)
            id_all = small[:, 0:3 * B].bitcast(U32).rearrange("p (t b) -> p t b", t=3)
            id_couple = small[:, 48:48 + 3 * J].bitcast(U32).rearrange("p (t j) -> p t j", t=3)

            def gather(k):
                rows, landed = (emb_second, gathered_second) if type(k) is int and k == 1 else (emb, gathered)
                if type(k) is not int or k > 1:
                    pool.wait_ge(emb_summed, 1 if type(k) is int and k == 2 else k)
                if type(k) is int:
                    index = id_all[:, :, k * J:(k + 1) * J]
                else:
                    index = id_couple
                    pool.tensor_copy(id_couple, id_all[:, :, bass.ds(k * J, J)]).then_inc(ids_staged, 1)
                    pool.wait_ge(ids_staged, k - 3)
                apart(pool)
                for t, table in enumerate((tok_table, pos_table, type_table)):
                    for j in range(J):
                        pool.indirect_dma_start(
                            out=rows[:, t, j, :], out_offset=None, in_=table,
                            in_offset=bass.IndirectOffsetOnAxis(ap=index[:, t, j:j + 1], axis=0),
                        ).then_inc(landed, 16)

            def scale_shift(k):
                part = hidden[:, bass.ds(k * J, J), :]
                pool.wait_ge(emb_normed, k + 1)
                pool.tensor_tensor(part, part, gam.unsqueeze(1).to_broadcast([P, J, D]), ALU.mult)\
                    .then_inc(scaled, 1)
                pool.wait_ge(scaled, k + 1)
                apart(pool)
                pool.tensor_tensor(part, part, bet.unsqueeze(1).to_broadcast([P, J, D]), ALU.add)\
                    .then_inc(hidden_ready, 1)

            def body(c):
                if not runs_self(c):
                    return
                diagonal(pool, c, 1, 1, diag_high)
                if type(c) is not int or c < NC - 3:
                    gather(c + 3)
                if runs_embed(c):
                    scale_shift(c + 2)
                if runs_next(c):
                    diagonal(pool, c + 1, 0, 1, diag_high)

            gather(0)
            gather(1)
            scale_shift(0)
            gather(2)
            scale_shift(1)
            diagonal(pool, 0, 0, 1, diag_high)
            couples(pool, body, peeled=3)

            wait_free(pool, "XS~", NC)

            def stage(i, u):
                if type(i) is int:
                    return
                pool.wait_ge(w1_used, 2 * i + (u - 1))
                pool.tensor_copy(staged[u], slots_t[:, :, bass.ds(i * SLOTS + GP * u, GP), :])\
                    .then_inc(slots_staged, 1)

            groups(pool, stage)

        @block.tensor
        def _(pe):
            pe.wait_ge(consts_ready, 7)

            def project(stage, c):
                bank, before = shared(stage, c)
                to = psum[:, SHARED_BANK + bank, :]
                if type(before) is not int or before > 0:
                    pe.wait_ge(shared_free[bank], before)
                if stage == "XT'":
                    pe.wait_ge(xa_ready, 1 if c is None else c + 2)
                    for half in range(2):
                        for j in range(J):
                            mm = turn(pe, to[0:HD, (half * J + j) * S:(half * J + j + 1) * S],
                                      xa[:, j, half * HD:(half + 1) * HD], P)
                elif stage[:2] == "QK":
                    wait_free(pe, "XT'", c)
                    for half in range(2):
                        at = int(stage[2]) * D + half * HD
                        for k in range(2):
                            mm = pe.matmul(to[0:HD, half * J * S:(half + 1) * J * S], w_qkv[0:HD, k, at:at + HD],
                                           xa_t[0:HD, k, :], start=(k == 0), stop=(k == 1))
                else:
                    for j in range(J):
                        for k in range(2):
                            mm = pe.matmul(to[:, j * D:(j + 1) * D], xa_t[0:HD, k, j * S:(j + 1) * S],
                                           w_qkv[0:HD, k, 2 * D:3 * D], start=(k == 0), stop=(k == 1))
                mm.then_inc(shared_full[bank], 1)

            def scores(c, j):
                b = c * J + j
                if j == 0:
                    pe.wait_ge(qk_copied, 2 * (c + 1))
                for m, (bank, g, h0, n) in enumerate([(0, 0, 0, 4), (1, 0, 4, 2), (1, 1, 0, 2), (2, 1, 2, 4)]):
                    pe.wait_ge((diag_low, diag_high)[g], b + 1)
                    if not first(b) and m != 2:
                        pe.wait_ge(squared, 3 * b + (bank - 2))
                    at = {0: 0, 1: 0, 2: 2 * S, 3: 0}[m]
                    pe.matmul(psum[:, bank, at:at + n * S], k_t[0:HD, g, j * S:(j + 1) * S],
                              q_diag[0:HD, g, h0:h0 + n, :], start=True, stop=True,
                              skip_group_check=True).then_inc(scores_done, 1)

            def weigh(c, j):
                b = c * J + j
                if not first(b):
                    pe.wait_ge(pv_copied, b)
                if j == 0:
                    wait_free(pe, "V", c)
                for h in range(H):
                    if h % 4 == 0:
                        pe.wait_ge(masked, 3 * b + (h // 4 + 1))
                    at = 32 * (h % 4)
                    mm = pe.matmul(psum[at:at + 32, PV_BANK, (h // 4) * S:(h // 4 + 1) * S], v_aug[:, j, h, :],
                                   probs[:, j, h, :], start=True, stop=True, skip_group_check=True)
                mm.then_inc(pv_done, 1)

            def turn_y(c, j):
                b = c * J + j
                pe.wait_ge(pv_copied, b + 1)
                if not first(b):
                    pe.wait_ge(yn_copied, b)
                for k in range(3):
                    mm = turn(pe, psum[:, Y_BANK, k * S:(k + 1) * S], pv_sb[:, k * S:(k + 1) * S], P)
                mm.then_inc(y_turned, 1)

            def turn_yn(c, j):
                pe.wait_ge(y_normed, c * J + (j + 1))
                for k in range(2):
                    mm = turn(pe, psum[0:HD, Y_BANK, k * S:(k + 1) * S], yn[:, k * HD:(k + 1) * HD], P)
                mm.then_inc(yn_turned, 1)

            def project_out(c, j):
                b = c * J + j
                pe.wait_ge(yn_copied, b + 1)
                if not first(b):
                    pe.wait_ge(attended, b)
                for k in range(2):
                    mm = pe.matmul(psum[:, WO_BANK, 0:D], yn_t[0:HD, k, :], w_o[:, k, :],
                                   start=(k == 0), stop=(k == 1))
                mm.then_inc(wo_done, 1)

            def route(stage, c):
                bank, before = shared(stage, c)
                to = psum[:, SHARED_BANK + bank, :]
                pe.wait_ge(shared_free[bank], before)
                if stage == "XN~":
                    pe.wait_ge(xn_ready, c)
                    for half in range(2):
                        for j in range(J):
                            mm = turn(pe, to[0:HD, (half * J + j) * S:(half * J + j + 1) * S],
                                      xn[:, j, half * HD:(half + 1) * HD], P)
                elif stage == "LT~":
                    wait_free(pe, "XN~", c)
                    for j in range(J):
                        for k in range(2):
                            mm = pe.matmul(to[NE * j:NE * (j + 1), 0:S], phi_n2[0:HD, k, :],
                                           xn_t[0:HD, k, j * S:(j + 1) * S], start=(k == 0), stop=(k == 1),
                                           skip_group_check=True)
                elif stage == "LN~":
                    wait_free(pe, "LT~", c)
                    mm = turn(pe, to[:, 0:P], log_t, P)
                elif stage == "DT~":
                    pe.wait_ge(disp_ready, c)
                    mm = turn(pe, to[:, 0:P], disp, P)
                elif stage == "XS~":
                    wait_free(pe, "DT~", c)
                    for j in range(J):
                        even, oddn = disp_t[:, j, 0:NE:2], disp_t[:, j, 1:NE:2]
                        for rows, tile, lo, hi, rhs in ((slice(0, P), 0, 0, P, even), (slice(0, P), 1, D - P, D, oddn),
                                                        (slice(0, NE), 2, P, D, even), (slice(NE, P), 2, 0, D - P, oddn)):
                            at = (tile * J + j) * NPAIR
                            mm = pe.matmul(to[rows, at:at + NPAIR], xn[:, j, lo:hi], rhs,
                                           start=True, stop=True, skip_group_check=True)
                else:
                    pe.wait_ge(comb_ready, c)
                    for j in range(J):
                        mm = turn(pe, to[:, j * S:(j + 1) * S], comb[:, j].rearrange("p r n -> p (r n)"), P)
                mm.then_inc(shared_full[bank], 1)

            attend = {"S": scores, "PV": weigh, "YT": turn_y, "YN": turn_yn, "WO": project_out}

            def body(c):
                for stage in ORDER:
                    if not runs(stage, c):
                        continue
                    if "'" in stage or stage == "V":
                        project(stage, c)
                    elif "~" in stage:
                        route(stage, c)
                    else:
                        attend[stage[:-1]](c, int(stage[-1]))

            pe.wait_ge(ids_fixed, 1)
            for t in range(3):
                mm = turn(pe, psum[:, Y_BANK, t * B:(t + 1) * B], ids_f[0:B, t, :], B)
            mm.then_inc(ids_turned, 1)
            pe.wait_ge(phi_squared, 1)
            for c in range(2):
                mm = pe.matmul(psum[0:HD, WO_BANK, 0:NE], ones[0:HD, :], phi_sq[0:HD, c, :],
                               start=(c == 0), stop=(c == 1))
            mm.then_inc(phi_summed, 1)
            pe.wait_ge(b1_loaded, 16)
            for t in range(KT2):
                mm = turn(pe, psum[:, PV_BANK, t * NE:(t + 1) * NE], b1_sb[0:NE, t:F:KT2], NE)
            mm.then_inc(b1_turned, 1)

            pe.wait_ge(wqkv_loaded, 48)
            for stage in PROJECT:
                project(stage, None)
            pe.wait_ge(wo_loaded, 16)
            pe.wait_ge(phi_ready, 1)
            pe.wait_ge(b1_ready, 1)
            couples(pe, body)

            def combine_early():
                pe.wait_ge(b2_spread, 1)
                pe.wait_ge(y_loaded, 16)
                pe.wait_ge(weights_spread, 2)
                pe.wait_ge(y_ready, NG - 1)
                for c in range(NC):
                    if c >= 3:
                        pe.wait_ge(early_added, c - 2)
                    for j in range(J):
                        b = c * J + j
                        to = psum[:, 5 + c % 3, j * D:(j + 1) * D]
                        pe.matmul(to, combine_t[:, b, :], slot_out[:, b, :], start=True, stop=False)
                        mm = pe.matmul(to, spread_weights[0][:, b, :], y_sb[0], start=False, stop=True)
                    mm.then_inc(early_combined, 1)

            def group(i, u):
                g = 2 * i + u
                if is_group(i, u, NG - 1):
                    combine_early()
                if type(i) is not int:
                    pe.wait_ge(slots_staged, g - 1)
                elif g == 0:
                    wait_free(pe, "XS~", NC)
                for k in range(GP):
                    pe.wait_ge(w1_loaded[GP * u + k], 16 * (i + 1))
                for kt in range(KT1):
                    for half in range(2):
                        for k in range(GP):
                            columns = slots_t[:, kt, g * GP + k, :] if type(i) is int else staged[u][:, kt, k, :]
                            mm = pe.matmul(psum[32 * k:32 * k + 32, half, 0:F // 2], columns,
                                           w1_slot(GP * u + k)[:, kt, half * (F // 2):(half + 1) * (F // 2)],
                                           start=(kt == 0), stop=(kt == KT1 - 1), skip_group_check=True)
                mm.then_inc(w1_used, 1)
                pe.wait_ge(h_copied, 2 * g + 2)
                for t in range(KT2):
                    mm = turn(pe, psum[:, 2 + t // 4, (t % 4) * P:(t % 4 + 1) * P], h_sb[:, t, :], P)
                    if t in (3, KT2 - 1):
                        mm.then_inc(h_turned, 1)
                if u or not first(i):
                    pe.wait_ge(y_ready, g)
                for t in range(KT2):
                    if t in (0, KT2 // 2):
                        for k in range(GP):
                            pe.wait_ge(w2_loaded[t // (KT2 // 2)][GP * u + k], 16 * (i + 1))
                    if t in (0, 4):
                        pe.wait_ge(act_ready, 2 * g + (1 if t == 0 else 2))
                    for k in range(GP):
                        mm = pe.matmul(psum[32 * k:32 * k + 32, 4, 0:2 * D], act_t[:, t, 32 * k:32 * k + 32],
                                       w2_slot(GP * u + k)[:, :, t, :], start=(t == 0), stop=(t == KT2 - 1),
                                       skip_group_check=True)
                mm.then_inc(w2_used, 1)

            groups(pe, group)

            pe.wait_ge(y_ready, NG)
            pe.wait_ge(early_added, NC)
            for c in range(NC):
                for j in range(J):
                    mm = pe.matmul(psum[:, c, j * D:(j + 1) * D], spread_weights[1][:, c * J + j, :], y_sb[1],
                                   start=True, stop=True)
                mm.then_inc(combined, 1)

        @block.vector
        def _(dve):
            BEFORE, BODY = 81, 32
            base, done = [0], [0]

            def tick(ins):
                done[0] += 1
                ins.then_inc(vec_step, 1)

            def settle():
                dve.wait_ge(vec_step, base[0] + done[0])

            def step(ins):
                tick(ins)
                settle()

            def rsqrt(y, v, t, batch=None):
                tick(dve.tensor_scalar(y.bitcast(I32), v.bitcast(I32), 1, None, ALU.logical_shift_right))
                if batch is not None:
                    diagonal(dve, batch[0], batch[1] + 1, 0, diag_low)
                settle()
                step(dve.tensor_scalar(y.bitcast(I32), y.bitcast(I32), -1.0, MAGIC, ALU.mult, ALU.add))
                for k in range(3):
                    step(dve.scalar_tensor_tensor(out=t, in0=v, scalar=-0.5, in1=y, op0=ALU.mult, op1=ALU.mult))
                    tick(dve.tensor_tensor(t, t, y, ALU.mult))
                    if batch is not None:
                        mask_scores(batch[0], batch[1], k)
                    settle()
                    step(dve.scalar_tensor_tensor(out=y, in0=t, scalar=1.5, in1=y, op0=ALU.add, op1=ALU.mult))

            EMB, ATT, ROU = 0, J, 2 * J
            stats = small[:, 60:96].rearrange("p (j s) -> p j s", s=6)
            mv = small[:, 96:108].rearrange("p (j s) -> p j s", s=2)
            vs, rs, tmp = small[:, 108:116], small[:, 116:124], small[:, 124:132]
            max_d, den_d, rec_d = small[:, 132:133], small[:, 133:134], small[:, 134:135]
            max_c, den_c, rec_c = small[:, 136:138], small[:, 138:140], small[:, 140:142]
            den_y, rec_y = small[:, 142:154], small[:, 154:166]

            def statistics(e, a, r):
                def bn(at, rows):
                    for j in range(J):
                        ins = dve.bn_stats(stats[:, at + j, :], rows(j))
                    return ins

                def row(k):
                    return lambda j: hidden[:, bass.ds(k * J + j, 1), :]

                for k, done_rows in ((e, emb_normed), (a, xa_ready), (r, xn_ready)):
                    if k is not None and not first(k):
                        dve.wait_ge(done_rows, k)
                if e is not None:
                    if type(e) is int and e == 1:
                        rows3 = emb_second
                        dve.wait_ge(gathered_second, 16 * 3 * J)
                    else:
                        rows3 = emb
                        dve.wait_ge(gathered, 16 * 3 * J * (1 if first(e) else e))
                    tick(dve.tensor_tensor(emb_sum, rows3[:, 0], rows3[:, 1], ALU.add))
                if a is not None:
                    dve.wait_ge(hidden_ready, a + 1)
                    apart(dve)
                    ins = bn(ATT, row(a))
                if e is not None:
                    settle()
                    dve.tensor_tensor(emb_sum, emb_sum, rows3[:, 2], ALU.add).then_inc(emb_summed, 1)
                if r is not None:
                    dve.wait_ge(attended, J * (r + 1))
                    apart(dve)
                    ins = bn(ROU, row(r))
                if e is not None:
                    dve.wait_ge(emb_summed, e + 1)
                    apart(dve)
                    ins = bn(EMB, lambda j: emb_sum[:, j, :])
                step(ins)
                apart(dve)
                for at, k in ((ATT, a), (ROU, r), (EMB, e)):
                    if k is not None:
                        for j in range(J):
                            ins = dve.bn_aggr(mv[:, at + j, :], stats[:, at + j, :])
                step(ins)
                if e is not None:
                    tick(dve.tensor_scalar(vs[:, EMB:EMB + J], mv[:, EMB:EMB + J, 1], 1e-12, None, ALU.add))
                if a is not None:
                    tick(dve.tensor_scalar(vs[:, ATT:ATT + J], mv[:, ATT:ATT + J, 1], 1e-5, None, ALU.add))
                if r is not None:
                    tick(dve.tensor_scalar(vs[:, ROU:ROU + J], mv[:, ROU:ROU + J, 1], 1e-5, None, ALU.add))
                    tick(dve.tensor_scalar(vs[:, ROU + J:], mv[:, ROU:ROU + J, 1], float(D), None, ALU.mult))
                settle()

            def normalise(e, a, r, here=None):
                def centre(k, out, source, at, j):
                    return dve.tensor_scalar(out, source, mv[:, at + j, 0:1], rs[:, at + j:at + j + 1],
                                             ALU.subtract, ALU.mult)

                def attention_row(j):
                    if a is not None:
                        ins = centre(a, xa[:, j:j + 1, :], hidden[:, bass.ds(a * J + j, 1), :], ATT, j)
                        if j == J - 1:
                            ins.then_inc(xa_ready, 1)

                def embedded_row(j):
                    if e is not None:
                        ins = centre(e, hidden[:, bass.ds(e * J + j, 1), :], emb_sum[:, j:j + 1, :], EMB, j)
                        if j == J - 1:
                            ins.then_inc(emb_normed, 1)

                rsqrt(rs, vs, tmp, None if here is None else (here, 0))
                if r is None:
                    for row in (attention_row, embedded_row):
                        for j in range(J):
                            row(j)
                    return
                length, rstd_r, inverse = tmp[:, 0:J], rs[:, ROU:ROU + J], tmp[:, J:2 * J]
                tick(dve.tensor_tensor(length, vs[:, ROU + J:], rs[:, ROU + J:], ALU.mult))
                attention_row(0)
                settle()
                tick(dve.tensor_tensor(length, length, rstd_r, ALU.mult))
                attention_row(1)
                settle()
                tick(dve.tensor_scalar(length, length, 1e-12, None, ALU.max))
                embedded_row(0)
                settle()
                tick(dve.reciprocal(inverse, length))
                embedded_row(1)
                settle()
                step(dve.tensor_tensor(rstd_r, rstd_r, inverse, ALU.mult))
                for j in range(J):
                    ins = centre(r, xn[:, j:j + 1, :], hidden[:, bass.ds(r * J + j, 1), :], ROU, j)
                ins.then_inc(xn_ready, 1)

            def mask_scores(c, j, k):
                part = probs[:, j, 4 * k:4 * k + 4, :]
                dve.wait_ge(squared, 3 * (c * J + j) + (k + 1))
                dve.scalar_tensor_tensor(out=part, in0=part, scalar=1.0, in1=mask.unsqueeze(1).to_broadcast([P, 4, S]),
                                         op0=ALU.add, op1=ALU.mult).then_inc(masked, 1)

            heads = psum[:, Y_BANK, 0:3 * S].rearrange("p (h e) -> p h e", e=32)

            def invert_y(c, j):
                dve.wait_ge(y_turned, c * J + (j + 1))
                step(dve.tensor_scalar(den_y, heads[:, :, FD], 2e-12, None, ALU.add))
                tick(dve.reciprocal(rec_y, den_y))

            def normalise_y(c, j):
                settle()
                dve.tensor_tensor(yn.rearrange("p (h e) -> p h e", e=FD), heads[:, :, 0:FD],
                                  rec_y.unsqueeze(2).to_broadcast([P, H, FD]), ALU.mult).then_inc(y_normed, 1)

            def add_attention(c, j):
                b = c * J + j
                dve.wait_ge(wo_done, b + 1)
                row = hidden[:, bass.ds(b, 1), :]
                dve.tensor_tensor(row, row, psum[:, WO_BANK, 0:D].unsqueeze(1), ALU.add).then_inc(attended, 1)

            def dispatch_max(c):
                bank, before = shared("LT~", c)
                dve.wait_ge(shared_full[bank], before + 1)
                dve.tensor_reduce(max_d, psum[:, SHARED_BANK + bank, 0:S], AX.X, ALU.max, negate=True)\
                    .then_inc(max_d_ready, 1)

            def dispatch_norm(c):
                dve.wait_ge(exp_d_ready, c)
                step(dve.reciprocal(rec_d, den_d))
                dve.tensor_scalar(disp, exp_d, rec_d, None, ALU.mult).then_inc(disp_ready, 1)

            def combine_max(c):
                bank, before = shared("LN~", c)
                dve.wait_ge(shared_full[bank], before + 1)
                logits = psum[:, SHARED_BANK + bank, 0:P].rearrange("p (j n) -> p j n", j=J)
                step(dve.tensor_reduce(max_c, logits, AX.X, ALU.max))
                step(dve.tensor_tensor(log_c, logits, max_c.unsqueeze(2).to_broadcast([P, J, NE]), ALU.subtract))
                dve.sem_inc(shared_free[bank], 1)
                dve.sem_inc(log_c_ready, 1)

            def combine_norm(c):
                dve.wait_ge(exp_c_ready, c)
                step(dve.tensor_reduce(den_c, exp_c, AX.X, ALU.add))
                step(dve.reciprocal(rec_c, den_c))
                dve.tensor_tensor(comb, exp_c.unsqueeze(2).to_broadcast([P, J, 2, NE]),
                                  rec_c.unsqueeze(2).unsqueeze(3).to_broadcast([P, J, 2, NE]), ALU.mult)\
                    .then_inc(comb_ready, 1)

            def body(c):
                if type(c) is not int:
                    assert done[0] == BEFORE, done[0]
                    base[0], done[0] = c * BODY + (BEFORE - BODY), 0
                here, prev = runs_self(c), runs_prev(c)
                those = (c + 2 if runs_embed(c) else None, c + 1 if runs_next(c) else None, c - 1 if prev else None)
                if not runs_embed(c):
                    dve.wait_ge(emb_normed, NC)
                if not runs_next(c):
                    dve.wait_ge(xa_ready, NC)
                statistics(*those)
                if first(c):
                    diagonal(dve, 0, 0, 0, diag_low)
                normalise(*those, c if here else None)
                if here:
                    for k in range(3):
                        mask_scores(c, 1, k)
                    invert_y(c, 0)
                if prev:
                    dispatch_max(c)
                if here:
                    normalise_y(c, 0)
                if prev:
                    dispatch_norm(c)
                    combine_max(c)
                if here:
                    add_attention(c, 0)
                    invert_y(c, 1)
                    normalise_y(c, 1)
                if runs_next(c):
                    diagonal(dve, c + 1, 0, 0, diag_low)
                if prev:
                    combine_norm(c)
                if here:
                    add_attention(c, 1)
                if type(c) is not int:
                    assert done[0] == BODY, done[0]
                    base[0], done[0] = BEFORE + (NC - 3) * BODY, 0

            dve.memset(vs, 1.0).then_inc(vec_step, 1)
            done[0] += 1
            dve.wait_ge(ids_loaded, 32)
            raw = ids.bitcast(I32)
            step(dve.tensor_copy(ids_f[0:B, 0, :], raw[0:B, 0:S]))
            step(dve.tensor_copy(ids_f[0:B, 2, :], raw[0:B, S:2 * S]))
            step(dve.tensor_copy(ids_f[0:B, 1, :], ids_f[0:B, 0, :]))
            for t, n in enumerate(TABLES):
                f = ids_f[0:B, t, :]
                step(dve.tensor_scalar(ids_w[0:B, :], f, 0.0, float(n), ALU.is_lt, ALU.mult))
                step(dve.tensor_tensor(f, f, ids_w[0:B, :], ALU.add))
                step(dve.tensor_scalar(f, f, 0.0, float(n - 1), ALU.max, ALU.min))
            dve.sem_inc(ids_fixed, 1)
            dve.wait_ge(ids_turned, 1)
            dve.tensor_copy(small[:, 0:3 * B].bitcast(U32), psum[:, Y_BANK, 0:3 * B]).then_inc(ids_ready, 1)
            dve.wait_ge(consts_ready, 7)
            step(dve.tensor_scalar(odd, odd, 4, 1, ALU.logical_shift_right, ALU.bitwise_and))

            dve.wait_ge(phi_loaded, 32)
            dve.tensor_tensor(phi_sq[0:HD], phi_sb[0:HD], phi_sb[0:HD], ALU.mult).then_inc(phi_squared, 1)
            dve.wait_ge(phi_summed, 1)
            n2, r, t = (phi_w[0:HD, i * NE:(i + 1) * NE] for i in range(3))
            step(dve.tensor_copy(n2, psum[0:HD, WO_BANK, 0:NE]))
            rsqrt(r, n2, t)
            step(dve.tensor_tensor(t, n2, r, ALU.mult))
            step(dve.tensor_scalar(t, t, 1e-12, None, ALU.max))
            step(dve.reciprocal(r, t))
            step(dve.tensor_scalar(r, r, phi_w[0:HD, 3 * NE:3 * NE + 1], None, ALU.mult))
            dve.tensor_tensor(phi_n2[0:HD], phi_sb[0:HD], r.unsqueeze(1).to_broadcast([HD, 2, NE]), ALU.mult)\
                .then_inc(phi_ready, 1)
            dve.wait_ge(b1_turned, 1)
            dve.tensor_copy(b1_t, psum[:, PV_BANK, 0:KT2 * NE].rearrange("p (t n) -> p t n", t=KT2))\
                .then_inc(b1_ready, 1)

            statistics(0, None, None)
            normalise(0, None, None)
            statistics(1, 0, None)
            normalise(1, 0, None)
            couples(dve, body)

            def spread_last_weights():
                dve.wait_ge(weights_loaded, 16)
                step(dve.tensor_reduce(batch_of_row, ident.rearrange("p (e b) -> p b e", b=B), AX.X, ALU.add))
                for u in range(2):
                    dve.tensor_tensor(spread_weights[u], last_weights[:, u:u + 1, :].to_broadcast([P, B, S]),
                                      batch_of_row.unsqueeze(2).to_broadcast([P, B, S]), ALU.mult)\
                        .then_inc(weights_spread, 1)

            def add(c, bank, ready, done_adding):
                dve.wait_ge(ready, c + 1)
                rows = hidden[:, c * J:(c + 1) * J, :]
                dve.tensor_tensor(rows, rows, psum[:, bank, 0:J * D].rearrange("p (j d) -> p j d", j=J), ALU.add)\
                    .then_inc(done_adding, 1)

            def group(i, u):
                g = 2 * i + u
                if is_group(i, u, NG - 1):
                    for c in range(NC):
                        add(c, 5 + c % 3, early_combined, early_added)
                dve.wait_ge(w1_used, g + 1)
                dve.tensor_copy(h_sb[:, :, P // 2:P].rearrange("p t c -> p c t"),
                                psum[:, 1, 0:F // 2].rearrange("p (c t) -> p c t", t=KT2)).then_inc(h_copied, 1)
                for part, (t0, t1) in enumerate(((0, 4), (4, KT2))):
                    dve.wait_ge(h_turned, 2 * g + (part + 1))
                    dve.tensor_tensor(
                        h_t[:, t0:t1], psum[:, 2 + part, 0:(t1 - t0) * P].rearrange("p (t e b) -> p t e b", e=G, b=B),
                        b1_t[:, t0:t1, bass.ds(g * G, G)].unsqueeze(3).to_broadcast([P, t1 - t0, G, B]),
                        ALU.add).then_inc(bias_added, 1)
                if is_group(i, u, 0):
                    dve.wait_ge(ahead_loaded, 16)
                    dve.tensor_copy(w1_slot(0), ahead).then_inc(w1_loaded[0], 16)
                if is_group(i, u, NG - 2):
                    spread_last_weights()
                dve.wait_ge(y_low, g + 1)
                apart(dve)
                dve.copy_predicated(y_sb[u], odd.to_broadcast([P, D]), psum[:, 4, D:2 * D]).then_inc(y_ready, 1)
                if is_group(i, u, 1):
                    dve.wait_ge(b2_loaded, 16)
                    dve.wait_ge(w1_loaded[0], 32)
                    dve.tensor_copy(slot_out[NE:P], b2_rows.unsqueeze(1).to_broadcast([NE, B, D]))\
                        .then_inc(b2_spread, 1)
                    dve.memset(slot_out[NE // 2:NE], 0.0).then_inc(rows_zeroed, 1)

            groups(dve, group)

            dve.wait_ge(early_added, NC)
            for c in range(NC):
                add(c, c, combined, added)

        @block.scalar
        def _(act):
            def evacuate(stage, c):
                if c is not None and not runs(stage, c):
                    return
                bank, before = shared(stage, c)
                full = psum[:, SHARED_BANK + bank, :]
                act.wait_ge(shared_full[bank], before + 1)
                if stage == "XT'":
                    ins = act.copy(xa_t[0:HD], full[0:HD, :].rearrange("p (h m) -> p h m", h=2))
                elif stage[:2] == "QK":
                    n = int(stage[2])
                    act.copy((q_t, k_t)[n][0:HD], full[0:HD, :].rearrange("p (h m) -> p h m", h=2))\
                        .then_inc(qk_copied, 1)
                    act.wait_ge(qk_copied, n + 1 if c is None else 2 * (c + 1) + (n + 1))
                    act.sem_inc(shared_free[bank], 1)
                    return
                elif stage == "V":
                    ins = act.copy(v_aug[:, :, :, 0:FD], full[:, 0:J * D].rearrange("p (j h e) -> p j h e", j=J, e=FD))
                elif stage == "XN~":
                    ins = act.copy(xn_t[0:HD], full[0:HD, :].rearrange("p (h m) -> p h m", h=2))
                elif stage == "DT~":
                    ins = act.copy(disp_t, full[:, 0:P].rearrange("p (j n) -> p j n", j=J))
                elif stage == "XS~":
                    part = full[:, 0:3 * J * NPAIR].rearrange("p (t j n) -> p t n j", t=3, j=J)
                    even, oddn = bass.ds(c * J - J, J), bass.ds(c * J + (B - J), J)
                    act.copy(slots_t[:, 0, :, even], part[:, 0])
                    act.copy(slots_t[:, 2, :, oddn], part[:, 1])
                    act.copy(slots_t[0:NE, 1, :, even], part[0:NE, 2])
                    ins = act.copy(slots_t[NE:P, 1, :, oddn], part[NE:P, 2])
                else:
                    ins = act.copy(combine_t[:, bass.ds(c * J - J, J), :],
                                   full[:, 0:J * S].rearrange("p (j m) -> p j m", j=J))
                ins.then_inc(shared_free[bank], 1)

            def square(c, j):
                b = c * J + j
                for k, ready in enumerate((1, 3, 4)):
                    act.wait_ge(scores_done, 4 * b + ready)
                    act.activation(probs[:, j, 4 * k:4 * k + 4, :],
                                   psum[:, k, :].rearrange("p (h m) -> p h m", h=4), ACT.Square,
                                   bias=1.0, scale=0.25).then_inc(squared, 1)

            def copy_pv(c, j):
                act.wait_ge(pv_done, c * J + (j + 1))
                act.copy(pv_sb, psum[:, PV_BANK, 0:3 * S]).then_inc(pv_copied, 1)

            def copy_yn(c, j):
                act.wait_ge(yn_turned, c * J + (j + 1))
                act.copy(yn_t[0:HD], psum[0:HD, Y_BANK, 0:2 * S].rearrange("p (c m) -> p c m", c=2))\
                    .then_inc(yn_copied, 1)

            def dispatch_exp(c):
                if not runs_prev(c):
                    return
                bank, before = shared("LT~", c)
                logits = psum[:, SHARED_BANK + bank, 0:S]
                act.wait_ge(max_d_ready, c)
                act.activation(exp_d, logits, ACT.Exp, bias=max_d, accum_out=den_d).then_inc(exp_d_ready, 1)
                act.copy(log_t, logits).then_inc(shared_free[bank], 1)

            def combine_exp(c):
                if runs_prev(c):
                    act.wait_ge(log_c_ready, c)
                    act.activation(exp_c, log_c, ACT.Exp).then_inc(exp_c_ready, 1)

            def body(c):
                here = runs_self(c)
                if here:
                    square(c, 0)
                    evacuate("V", c)
                    if first(c):
                        act.wait_ge(emb_summed, 2)
                    square(c, 1)
                    copy_pv(c, 0)
                evacuate("XN~", c)
                dispatch_exp(c)
                if here:
                    copy_pv(c, 1)
                    copy_yn(c, 0)
                evacuate("XT'", c)
                combine_exp(c)
                evacuate("QK0'", c)
                evacuate("DT~", c)
                evacuate("QK1'", c)
                if here:
                    copy_yn(c, 1)
                evacuate("XS~", c)
                evacuate("CT~", c)

            max_d, den_d = small[:, 132:133], small[:, 133:134]
            act.wait_ge(consts_ready, 7)
            for stage in PROJECT:
                evacuate(stage, None)
            couples(act, body)

            def group(i, u):
                g = 2 * i + u
                if is_group(i, u, NG - 2):
                    for k in range(2):
                        act.wait_ge(y_stored[k], 16 * (NG // 2 - 1))
                    act.wait_ge(rows_zeroed, 1)
                    act.dma_start(slot_out[0:EARLY_NE], y_dram.rearrange("(n b) d -> n b d", b=B))\
                        .then_inc(y_loaded, 16)
                act.wait_ge(w1_used, g + 1)
                act.copy(h_sb[:, :, 0:P // 2].rearrange("p t c -> p c t"),
                         psum[:, 0, 0:F // 2].rearrange("p (c t) -> p c t", t=KT2)).then_inc(h_copied, 1)
                for part, (t0, t1) in enumerate(((0, 4), (4, KT2))):
                    act.wait_ge(bias_added, 2 * g + (part + 1))
                    act.activation(act_t[:, t0:t1, :], h_t[:, t0:t1].rearrange("p t e b -> p t (e b)"), ACT.Gelu)\
                        .then_inc(act_ready, 1)
                act.wait_ge(w2_used, g + 1)
                if not first(i):
                    act.wait_ge(y_stored[u], 16 * i)
                act.copy(y_sb[u], psum[:, 4, 0:D]).then_inc(y_low, 1)
                if is_group(i, u, NG - 2) or is_group(i, u, NG - 1):
                    return
                act.wait_ge(y_ready, g + 1)
                act.dma_start(y_dram[bass.ds(g * P, P), :], y_sb[u]).then_inc(y_stored[u], 16)

            groups(act, group)


_INS = ['x', 'mask_BS_i1_0', 'L0_tok_tok_table', 'L0_tok_pos_table', 'L0_tok_type_table', 'L0_tok_gamma',
        'L0_tok_beta', 'L0_attn_Wq', 'L0_attn_Wk', 'L0_attn_Wv', 'L0_attn_Wo', 'L0_ffn_phi', 'L0_ffn_scale',
        'L0_ffn_w1', 'L0_ffn_b1', 'L0_ffn_w2', 'L0_ffn_b2']
_OUT = ((16, 128, 192), 'float32')


def kernel(**inputs):
    import numpy as _np
    import concourse.bacc as _bacc
    from concourse import mybir as _mybir
    from concourse.bass_utils import run_bass_kernel_spmd as _run

    nc = _bacc.Bacc("TRN2", target_bir_lowering=False, num_devices=1)
    arrays, args = {}, []
    for name in _INS:
        a = _np.ascontiguousarray(inputs[name])
        arrays[f"in_{name}_dram"] = a
        args.append(nc.dram_tensor(f"in_{name}_dram", a.shape, _mybir.dt.from_np(a.dtype), kind="ExternalInput").ap())
    shape, dtype = _OUT
    args.append(nc.dram_tensor("out_0_dram", shape, _mybir.dt.from_np(_np.dtype(dtype)), kind="ExternalOutput").ap())
    tower_kernel(nc, *args)
    r = _run(nc, [arrays], core_ids=[0])
    return r.results[0]["out_0_dram"]
```
